# Optimizing a Trainium2 kernel written in Bass

```python
import numpy as np
import jax
import jax.numpy as jnp

def _softmax(x, axis=-1):
    return jax.nn.softmax(x, axis=axis)

def _gelu(x):
    return jax.nn.gelu(x, approximate=True)

def _silu(x):
    return jax.nn.silu(x)

def _sigmoid(x):
    return jax.nn.sigmoid(x)

def _layernorm(x, axis=-1, eps=1e-05):
    m = jnp.mean(x, axis=axis, keepdims=True)
    v = jnp.var(x, axis=axis, keepdims=True)
    return (x - m) / jnp.sqrt(v + eps)

def _scatter_add(tgt, idx, src, axis=0):
    return tgt.at[idx].add(src)

def _segment_sum(src, seg, n):
    return jax.ops.segment_sum(src, seg, n)
kernel_name = 'mk_adj_preln_d4_adj_r2_b0b21a'

def setup_inputs(seed: int=0):
    np.random.seed(seed)
    _w = jnp.asarray

    def _rec_inputs():
        import jax
        import jax.numpy as jnp
        _gk = jax.random.key(seed)
        x = -0.000929 + 1 * jax.random.normal(jax.random.fold_in(_gk, 1), (32, 256, 256), jnp.float32)
        _a = jax.random.bernoulli(jax.random.fold_in(_gk, 2), 0.0625, (256, 256))
        adj = _a.astype(jnp.int32)
        return (x, adj)
    x, adj = _rec_inputs()

    def _L0_gnn_setup():
        import jax, jax.numpy as jnp
        import numpy as np
        B, K, DIN, DOUT = (32, 64, 256, 256)
        key = jax.random.key(seed)
        k1, k2, k3, k4 = jax.random.split(key, 4)
        x = jax.random.normal(k1, (B, K, DIN), dtype=jnp.float32)
        adj = jax.random.randint(k2, (K, K), 0, 2, dtype=jnp.int32)
        W = jax.random.normal(k3, (DOUT, 2 * DIN), dtype=jnp.float32) * 0.02
        b = jax.random.normal(k4, (DOUT,), dtype=jnp.float32) * 0.02
        return {'x': x, 'adj': adj, 'W': W, 'b': b}
    _L0_gnn_all = _L0_gnn_setup()
    _L0_gnn_in = {k: v for k, v in _L0_gnn_all.items() if k in ('W', 'b')}
    del _L0_gnn_all

    def _L1_gnn_setup():
        import jax, jax.numpy as jnp
        import numpy as np
        B, N, D = (8, 1024, 256)
        NEG_SLOPE = 0.2
        key = jax.random.key(seed)
        k1, k2, k3, k4, k5 = jax.random.split(key, 5)
        x = jax.random.normal(k1, (B, N, D), dtype=jnp.float32)
        adj = jax.random.randint(k2, (N, N), 0, 2, dtype=jnp.int32)
        adj = jnp.maximum(adj, jnp.eye(N, dtype=jnp.int32))
        W = jax.random.normal(k3, (D, D), dtype=jnp.float32) * (1.0 / np.sqrt(D))
        a_src = jax.random.normal(k4, (D,), dtype=jnp.float32) * (1.0 / np.sqrt(D))
        a_dst = jax.random.normal(k5, (D,), dtype=jnp.float32) * (1.0 / np.sqrt(D))
        return {'x': x, 'adj': adj, 'W': W, 'a_src': a_src, 'a_dst': a_dst}
    _L1_gnn_all = _L1_gnn_setup()
    _L1_gnn_in = {k: v for k, v in _L1_gnn_all.items() if k in ('W', 'a_src', 'a_dst')}
    del _L1_gnn_all

    def _L2_gnn_setup():
        import jax, jax.numpy as jnp
        import numpy as np
        D_MODEL = 256
        NUM_HEADS = 8
        D_HEAD = D_MODEL // NUM_HEADS
        B, N = (4, 1024)
        key = jax.random.key(seed)
        ks = jax.random.split(key, 10)
        s = 1.0 / np.sqrt(D_MODEL)
        inp = {'h': jax.random.normal(ks[0], (B, N, D_MODEL), dtype=jnp.float32), 'adj': jax.random.randint(ks[1], (N, N), 0, 2, dtype=jnp.int32), 'Wq': jax.random.uniform(ks[2], (D_MODEL, D_MODEL), jnp.float32, -s, s), 'bq': jax.random.uniform(ks[3], (D_MODEL,), jnp.float32, -s, s), 'Wk': jax.random.uniform(ks[4], (D_MODEL, D_MODEL), jnp.float32, -s, s), 'bk': jax.random.uniform(ks[5], (D_MODEL,), jnp.float32, -s, s), 'Wv': jax.random.uniform(ks[6], (D_MODEL, D_MODEL), jnp.float32, -s, s), 'bv': jax.random.uniform(ks[7], (D_MODEL,), jnp.float32, -s, s), 'Wo': jax.random.uniform(ks[8], (D_MODEL, D_MODEL), jnp.float32, -s, s), 'bo': jax.random.uniform(ks[9], (D_MODEL,), jnp.float32, -s, s)}
        return inp
    _L2_gnn_all = _L2_gnn_setup()
    _L2_gnn_in = {k: v for k, v in _L2_gnn_all.items() if k in ('Wq', 'bq', 'Wk', 'bk', 'Wv', 'bv', 'Wo', 'bo')}
    del _L2_gnn_all

    def _L3_gnn_setup():
        import jax, jax.numpy as jnp
        import numpy as np
        LEAKY_ALPHA = 0.01
        NEG_INF = -1000000000.0
        LN_EPS = 1e-05

        def _gat_heads(x, adj, W, a):
            O = W.shape[-1]
            Wh = jnp.einsum('bnf,hfo->bhno', x, W)
            f1 = jnp.einsum('bhno,ho->bhn', Wh, a[:, :O])
            f2 = jnp.einsum('bhno,ho->bhn', Wh, a[:, O:])
            e = f1[:, :, :, None] + f2[:, :, None, :]
            e = jnp.where(e > 0, e, LEAKY_ALPHA * e)
            e = jnp.where(adj[None, None] > 0, e, NEG_INF)
            attn = jax.nn.softmax(e, axis=-1)
            return jnp.einsum('bhnm,bhmo->bhno', attn, Wh)
        key = jax.random.key(seed)
        ks = jax.random.split(key, 10)
        B, N, F_in, F_hid, H, F_out, D_ff = (8, 1024, 256, 256, 4, 256, 256)
        s = 0.05
        return {'enc_inputs': jax.random.normal(ks[0], (B, N, F_in), jnp.float32), 'adj': jax.random.randint(ks[1], (N, N), 0, 2, jnp.int32), 'W_heads': jax.random.normal(ks[2], (H, F_in, F_hid), jnp.float32) * s, 'a_heads': jax.random.normal(ks[3], (H, 2 * F_hid), jnp.float32) * s, 'W_out': jax.random.normal(ks[4], (H * F_hid, F_out), jnp.float32) * s, 'a_out': jax.random.normal(ks[5], (2 * F_out,), jnp.float32) * s, 'w1': jax.random.normal(ks[6], (F_out, D_ff), jnp.float32) * s, 'b1': jnp.zeros((D_ff,), jnp.float32), 'w2': jax.random.normal(ks[7], (D_ff, F_out), jnp.float32) * s, 'b2': jnp.zeros((F_out,), jnp.float32), 'ln_gamma': jnp.ones((F_out,), jnp.float32), 'ln_beta': jnp.zeros((F_out,), jnp.float32)}
    _L3_gnn_all = _L3_gnn_setup()
    _L3_gnn_in = {k: v for k, v in _L3_gnn_all.items() if k in ('W_heads', 'a_heads', 'W_out', 'a_out', 'w1', 'b1', 'w2', 'b2', 'ln_gamma', 'ln_beta')}
    del _L3_gnn_all
    return {'x': x, 'adj': adj, 'L0_gnn_W': _L0_gnn_in['W'], 'L0_gnn_b': _L0_gnn_in['b'], 'L1_gnn_W': _L1_gnn_in['W'], 'L1_gnn_a_src': _L1_gnn_in['a_src'], 'L1_gnn_a_dst': _L1_gnn_in['a_dst'], 'L2_gnn_Wq': _L2_gnn_in['Wq'], 'L2_gnn_bq': _L2_gnn_in['bq'], 'L2_gnn_Wk': _L2_gnn_in['Wk'], 'L2_gnn_bk': _L2_gnn_in['bk'], 'L2_gnn_Wv': _L2_gnn_in['Wv'], 'L2_gnn_bv': _L2_gnn_in['bv'], 'L2_gnn_Wo': _L2_gnn_in['Wo'], 'L2_gnn_bo': _L2_gnn_in['bo'], 'L3_gnn_W_heads': _L3_gnn_in['W_heads'], 'L3_gnn_a_heads': _L3_gnn_in['a_heads'], 'L3_gnn_W_out': _L3_gnn_in['W_out'], 'L3_gnn_a_out': _L3_gnn_in['a_out'], 'L3_gnn_w1': _L3_gnn_in['w1'], 'L3_gnn_b1': _L3_gnn_in['b1'], 'L3_gnn_w2': _L3_gnn_in['w2'], 'L3_gnn_b2': _L3_gnn_in['b2'], 'L3_gnn_ln_gamma': _L3_gnn_in['ln_gamma'], 'L3_gnn_ln_beta': _L3_gnn_in['ln_beta']}

def reference(x, adj, L0_gnn_W, L0_gnn_b, L1_gnn_W, L1_gnn_a_src, L1_gnn_a_dst, L2_gnn_Wq, L2_gnn_bq, L2_gnn_Wk, L2_gnn_bk, L2_gnn_Wv, L2_gnn_bv, L2_gnn_Wo, L2_gnn_bo, L3_gnn_W_heads, L3_gnn_a_heads, L3_gnn_W_out, L3_gnn_a_out, L3_gnn_w1, L3_gnn_b1, L3_gnn_w2, L3_gnn_b2, L3_gnn_ln_gamma, L3_gnn_ln_beta):
    import jax
    import jax.numpy as jnp

    def _L0_gnn_ref(x, adj, W, b):
        import jax, jax.numpy as jnp
        import numpy as np
        B, K, DIN, DOUT = (32, 64, 256, 256)
        Din = x.shape[-1]
        Wi, Wj = (W[:, :Din], W[:, Din:])
        mi = jnp.einsum('bkd,od->bko', x, Wi)
        mj = jnp.einsum('bkd,od->bko', x, Wj)
        a = adj.astype(x.dtype)
        deg = a.sum(axis=1)
        out = deg[None, :, None] * (mi + b) + jnp.einsum('ij,bjo->bio', a, mj)
        return out

    def _L1_gnn_ref(x, adj, W, a_src, a_dst):
        import jax, jax.numpy as jnp
        import numpy as np
        B, N, D = (8, 1024, 256)
        NEG_SLOPE = 0.2
        Wh = jnp.einsum('bnd,de->bne', x, W)
        e_src = jnp.einsum('bnd,d->bn', Wh, a_src)
        e_dst = jnp.einsum('bnd,d->bn', Wh, a_dst)
        logits = e_src[:, :, None] + e_dst[:, None, :]
        logits = jnp.where(logits >= 0, logits, NEG_SLOPE * logits)
        mask = (adj == 0)[None, :, :]
        logits = jnp.where(mask, -jnp.inf, logits)
        attn = jax.nn.softmax(logits, axis=-1)
        attn = jnp.nan_to_num(attn, nan=0.0)
        out = jnp.einsum('bnm,bmd->bnd', attn, Wh)
        return out

    def _L2_gnn_ref(h, adj, Wq, bq, Wk, bk, Wv, bv, Wo, bo):
        import jax, jax.numpy as jnp
        import numpy as np
        D_MODEL = 256
        NUM_HEADS = 8
        D_HEAD = D_MODEL // NUM_HEADS
        B, N = (4, 1024)
        b, n, _ = h.shape

        def split_heads(x):
            return x.reshape(b, n, NUM_HEADS, D_HEAD).transpose(0, 2, 1, 3)
        q = split_heads(h @ Wq.T + bq)
        k = split_heads(h @ Wk.T + bk)
        v = split_heads(h @ Wv.T + bv)
        scale = 1.0 / np.sqrt(D_HEAD)
        scores = jnp.einsum('bhqd,bhkd->bhqk', q, k) * scale
        mask = (adj == 0)[None, None, :, :]
        scores = jnp.where(mask, -jnp.inf, scores)
        attn = jax.nn.softmax(scores, axis=-1)
        out = jnp.einsum('bhqk,bhkd->bhqd', attn, v)
        out = out.transpose(0, 2, 1, 3).reshape(b, n, D_MODEL)
        return out @ Wo.T + bo

    def _L3_gnn_ref(enc_inputs, adj, W_heads, a_heads, W_out, a_out, w1, b1, w2, b2, ln_gamma, ln_beta):
        import jax, jax.numpy as jnp
        import numpy as np
        LEAKY_ALPHA = 0.01
        NEG_INF = -1000000000.0
        LN_EPS = 1e-05

        def _gat_heads(x, adj, W, a):
            O = W.shape[-1]
            Wh = jnp.einsum('bnf,hfo->bhno', x, W)
            f1 = jnp.einsum('bhno,ho->bhn', Wh, a[:, :O])
            f2 = jnp.einsum('bhno,ho->bhn', Wh, a[:, O:])
            e = f1[:, :, :, None] + f2[:, :, None, :]
            e = jnp.where(e > 0, e, LEAKY_ALPHA * e)
            e = jnp.where(adj[None, None] > 0, e, NEG_INF)
            attn = jax.nn.softmax(e, axis=-1)
            return jnp.einsum('bhnm,bhmo->bhno', attn, Wh)
        B, N, _ = enc_inputs.shape
        h = jax.nn.elu(_gat_heads(enc_inputs, adj, W_heads, a_heads))
        h = jnp.transpose(h, (0, 2, 1, 3)).reshape(B, N, -1)
        out = _gat_heads(h, adj, W_out[None], a_out[None])[:, 0]
        out = jax.nn.elu(out)
        ffn = jnp.maximum(out @ w1 + b1, 0.0) @ w2 + b2
        y = ffn + out
        mu = jnp.mean(y, axis=-1, keepdims=True)
        var = jnp.var(y, axis=-1, keepdims=True)
        return (y - mu) / jnp.sqrt(var + LN_EPS) * ln_gamma + ln_beta
    h = jnp.maximum(_layernorm(x, axis=-1), 0.0)
    x = x + _L0_gnn_ref(h, adj, L0_gnn_W, L0_gnn_b)
    h = jnp.maximum(_layernorm(x, axis=-1), 0.0)
    x = x + _L1_gnn_ref(h, adj, L1_gnn_W, L1_gnn_a_src, L1_gnn_a_dst)
    h = jnp.maximum(_layernorm(x, axis=-1), 0.0)
    x = x + _L2_gnn_ref(h, adj, L2_gnn_Wq, L2_gnn_bq, L2_gnn_Wk, L2_gnn_bk, L2_gnn_Wv, L2_gnn_bv, L2_gnn_Wo, L2_gnn_bo)
    h = jnp.maximum(_layernorm(x, axis=-1), 0.0)
    x = x + _L3_gnn_ref(h, adj, L3_gnn_W_heads, L3_gnn_a_heads, L3_gnn_W_out, L3_gnn_a_out, L3_gnn_w1, L3_gnn_b1, L3_gnn_w2, L3_gnn_b2, L3_gnn_ln_gamma, L3_gnn_ln_beta)
    return x

_drawn_inputs = setup_inputs


def setup_inputs(seed=0):
    import zlib

    import numpy as np

    out = dict(_drawn_inputs(seed))
    spreads = {'L3_gnn_b1': (0.0, 0.341),
     'L3_gnn_b2': (0.0, 0.1),
     'L3_gnn_ln_gamma': (1.0, 0.2),
     'L3_gnn_ln_beta': (0.0, 0.38)}
    factors = {'L1_gnn_a_src': 27.498,
     'L1_gnn_a_dst': 4.685,
     'L2_gnn_Wq': 8.0,
     'L2_gnn_bq': 64.0,
     'L2_gnn_Wk': 8.0,
     'L2_gnn_bk': 64.0,
     'L2_gnn_bv': 8.0,
     'L2_gnn_bo': 6.823,
     'L3_gnn_a_heads': 8.0,
     'L3_gnn_a_out': 8.0}
    for name, (base, spread) in spreads.items():
        noise = np.random.default_rng([zlib.crc32(name.encode()), seed]).standard_normal(out[name].shape)
        drawn = base * np.exp(spread * noise) if base else spread * noise
        out[name] = jnp.asarray(drawn.astype(out[name].dtype))
    for name, factor in factors.items():
        out[name] = (out[name] * factor).astype(out[name].dtype)
    return out
```

```python
import concourse.bass as bass
from concourse import mybir
from contextlib import ExitStack


def adj_preln_kernel(nc, x, adj, adj_t, L0_W_t, L0_b, L1_W, L1_a_src, L1_a_dst,
                     Wq_t, bq, Wk_t, bk, Wv_t, bv, Wo_t, bo,
                     W_heads, a_heads, W_out, a_out, w1, b1, w2, b2, gamma, beta, out):
    F32, F32R = mybir.dt.float32, mybir.dt.float32r
    F16, BF16, I32 = mybir.dt.float16, mybir.dt.bfloat16, mybir.dt.int32
    ALU, ACT, AX = mybir.AluOpType, mybir.ActivationFunctionType, mybir.AxisListType

    B, N, D = x.shape
    P = 128
    C = N // P
    assert N == D == 2 * P and B % 2 == 0
    HQ = 8
    DH = D // HQ
    HG = W_heads.shape[0]
    SCALE = float(DH) ** -0.5
    BIG = 1.0e30
    EPS = 1e-5
    SLOPE = [0.2] + [0.01] * (HG + 1)
    GOUT = HG + 1
    WC = D + 2
    VC = 3 * DH + 1
    S2 = (0, 1)
    BANK = 512
    PARTS = ((0, 0), (0, 1), (1, 0))
    LOOPS = B // 2

    ctx = ExitStack()
    with ctx:
        def sb(name, shape, dt=F32):
            return ctx.enter_context(nc.sbuf_tensor(name, shape, dt))

        def sem(name):
            return ctx.enter_context(nc.semaphore(name))

        sems = []

        def sem2(name):
            pair = [sem(f"{name}{s}") for s in S2]
            sems.extend(pair)
            return pair

        w0 = sb("w0", [P, 2, 2 * C, D], F32R)
        w1g = sb("w1g", [P, 2, C, WC], F32R)
        wq = sb("wq", [P, 2, C, D], F32R)
        wk = sb("wk", [P, 2, C, D], F32R)
        wv = sb("wv", [P, 2, C, D], F32R)
        wo = sb("wo", [P, 2, C, D], F32R)
        wh = sb("wh", [P, 2, HG * C, WC], F32R)
        wout = sb("wout", [P, 2, HG * C, WC], F32R)
        wf1 = sb("wf1", [P, 2, C, D], F32R)
        wf2 = sb("wf2", [P, 2, C, D], F32R)
        at = sb("at", [P, 2, C, N], F32R)
        maskp = sb("maskp", [P, C, N])
        mask3p = sb("mask3p", [P, C, N])
        deg = sb("deg", [P, C])
        has = sb("has", [P, C])
        degb = sb("degb", [P, C, D])
        bo_nan = sb("bo_nan", [P, C, D])
        bv_b = sb("bv_b", [P, D])
        b2_b = sb("b2_b", [P, D])
        gamma_b = sb("gamma_b", [P, D])
        beta_b = sb("beta_b", [P, D])
        bq_c = sb("bq_c", [P, C])
        bk_c = sb("bk_c", [P, C])
        b1_c = sb("b1_c", [P, C])
        ident = sb("ident", [P, P])
        ident16 = sb("ident16", [P, P], F16)
        pow_half = sb("pow_half", [P, C])

        def per(name, shape, dt=F32):
            return [sb(f"{name}_{s}", shape, dt) for s in S2]

        xin = per("xin", [P, C, D])
        xs = per("xs", [P, C, D])
        tb = per("tb", [P, C, N])
        e1 = per("e1", [P, C, N])
        e2 = per("e2", [P, C, N])
        pr = per("pr", [P, C, N])
        rb = per("rb", [P, C, N])
        fu = per("fu", [P, C, N])
        hT = per("hT", [P, 2, C, N], F32R)
        whs = [[sb(f"whs{k}_{s}", [P, 2, C, D], F32R) for k in range(2)] for s in S2]
        pT = per("pT", [P, 2, C, N], F32R)
        hid = per("hid", [P, 2, HG * C, N], F32R)
        v3 = per("v3", [P, C, HQ, VC], BF16)
        p16 = [[sb(f"p16{k}_{s}", [P, 2, C, N], F16) for k in range(2)] for s in S2]
        pT16 = per("pT16", [P, 2, C, N], F16)
        cols = per("cols", [P, C, 2])
        dmin = per("dmin", [P, C])
        zz = per("zz", [P, C])
        mm = per("mm", [P, C])
        bias1 = per("bias1", [P, C])
        bias2 = per("bias2", [P, C])
        psums = per("psums", [P, C])
        rs = per("rs", [P, C])
        hmin = [[sb(f"hmin{k}_{s}", [P, C]) for k in range(2)] for s in S2]
        rden = per("rden", [P, 2 * C])
        stats = per("stats", [P, C, 6])
        mv = per("mv", [P, C, 2])
        ve = per("ve", [P, C])
        rstd = per("rstd", [P, C])

        ps = [ctx.enter_context(nc.psum_tensor(f"ps{s}", [P, 4 * BANK], F32)) for s in S2]
        BA, BB, BC, BD = range(4)

        def bank(s, k, n=N):
            return ps[s][:, k * BANK:k * BANK + 2 * n].rearrange("p (c n) -> p c n", c=2)

        def wh_banks(s):
            return ps[s][:, 0:2 * BANK].rearrange("p (c n) -> p c n", c=2)

        def bank16(s, k):
            return ps[s][:, k * BANK:(k + 1) * BANK].bitcast(F16).rearrange("p (t c n) -> p t c n", t=2, c=C)

        def f(t):
            return t.bitcast(F32)

        def as_heads(t):
            return t[:].rearrange("p c (h d) -> p c h d", h=HQ)

        def v_part(s, k):
            return v3[s][:, :, :, k * DH:(k + 1) * DH]

        def l2_logits(s, h):
            return (tb, e1)[h % 2][s]

        def l2_probs(s, h):
            return (pr, e2)[h % 2][s]

        stored = sem("stored")

        stage = [tb[0], e1[0], e2[0], pr[0], rb[0], fu[0], tb[1], e1[1]]
        NST = len(stage)
        avec = [e2[1], pr[1], rb[1], fu[1], xs[0], xs[1]]

        def halves(w, k):
            return w[k * D:(k + 1) * D, :].rearrange("(c p) n -> p c n", p=P)

        units = [(halves(L0_W_t, 0), w0[:, :, 0:C, :], None), (halves(L0_W_t, 1), w0[:, :, C:2 * C, :], None),
                 (halves(L1_W, 0), w1g[:, :, :, :], 0),
                 (halves(Wq_t, 0), wq[:, :, :, :], None), (halves(Wk_t, 0), wk[:, :, :, :], None),
                 (halves(Wv_t, 0), wv[:, :, :, :], None), (halves(Wo_t, 0), wo[:, :, :, :], None)]
        units += [(halves(W_heads[h], 0), wh[:, :, C * h:C * h + C, :], 1 + h) for h in range(HG)]
        units += [(halves(W_out, h), wout[:, :, C * h:C * h + C, :], GOUT) for h in range(HG)]
        units += [(halves(w1, 0), wf1[:, :, :, :], None), (halves(w2, 0), wf2[:, :, :, :], None)]
        avecs = [(L1_a_src, L1_a_dst)] + [(a_heads[h, 0:D], a_heads[h, D:2 * D]) for h in range(HG)] \
            + [(a_out[0:D], a_out[D:2 * D])]
        NU = len(units)

        def bcast(v):
            return v.rearrange("(o n) -> o n", o=1).broadcast_to([P, v.shape[0]])

        def column(v):
            return v.rearrange("(c p) -> p c", p=P)

        staged = [sem(f"staged{k}") for k in range(NST)]
        small = sem("small")
        adj_in = sem("adj_in")
        split_hi = sem("split_hi")
        split_lo = sem("split_lo")
        scored = sem("scored")
        made = sem("made")
        pooled = sem("pooled")
        first_x = sem("first_x")
        wcol = sb("wcol", [P, NU, C, 2])
        junk = sb("junk", [P, D])
        adj_i, adjt_i, adj_f, adjt_f = (hT_alias for hT_alias in (
            xs[0], xs[1], tb[0], e1[0]))

        n_small = 0
        with nc.Block() as block:
            @block.sync
            def _(sp):
                sp.sem_inc(stored, 32)
                for s in S2:
                    sp.dma_start(xin[s][:], x[s].rearrange("(c p) d -> p c d", p=P)).then_inc(first_x, 16)
                for n, (src, _, _) in enumerate(units):
                    if n >= NST:
                        sp.wait_ge(split_lo, n - NST + 1)
                    sp.dma_start(stage[n % NST][:], src).then_inc(staged[n % NST], 16)
                sp.wait_ge(split_lo, NU)
                sp.dma_start(adj_i[:].bitcast(I32), adj.rearrange("(c p) n -> p c n", p=P)).then_inc(adj_in, 16)
                sp.dma_start(adjt_i[:].bitcast(I32), adj_t.rearrange("(c p) n -> p c n", p=P)).then_inc(adj_in, 16)
                sp.wait_ge(first_x, 32)

            @block.gpsimd
            def _(pool):
                pool.memset(ident[:], 0.0).then_inc(pooled, 1)
                pool.memset(pow_half[:], -0.5).then_inc(pooled, 1)
                for s in S2:
                    pool.memset(v3[s][:], 1.0).then_inc(pooled, 1)
                pool.wait_ge(pooled, 4)
                pool.affine_select(out=ident[:], in_=ident[:], compare_op=ALU.not_equal, fill=1.0, base=0,
                                   pattern=[[-1, P]], channel_multiplier=1).then_inc(pooled, 1)
                pool.wait_ge(pooled, 5)
                pool.tensor_copy(ident16[:], ident[:]).then_inc(pooled, 1)

            @block.scalar
            def _(act):
                for k, (a, b) in enumerate(avecs):
                    act.dma_start(avec[k][:, 0, :], bcast(a)).then_inc(small, 16)
                    act.dma_start(avec[k][:, 1, :], bcast(b)).then_inc(small, 16)
                for dst, v in ((bv_b, bv), (b2_b, b2), (gamma_b, gamma), (beta_b, beta)):
                    act.dma_start(dst[:], bcast(v)).then_inc(small, 16)
                act.dma_start(degb[:, 0, :], bcast(L0_b)).then_inc(small, 16)
                act.dma_start(bo_nan[:, 0, :], bcast(bo)).then_inc(small, 16)
                for dst, v in ((bq_c, bq), (bk_c, bk), (b1_c, b1)):
                    with nc.allow_non_contiguous_dma(reason="bias columns, once"):
                        act.dma_start(dst[:], column(v)).then_inc(small, 16)
                for n, (_, dst, _) in enumerate(units):
                    act.wait_ge(staged[n % NST], 16 * (n // NST + 1))
                    act.activation(dst[:, 0, :, 0:D], stage[n % NST][:], ACT.Copy).then_inc(split_hi, 1)

            @block.vector
            def _(dve):
                step = 0

                def chain(ins):
                    nonlocal step
                    step += 1
                    ins.then_inc(made, 1)
                    dve.wait_ge(made, step)

                dve.wait_ge(small, 16 * (2 * len(avecs) + 9))
                for n, (_, dst, g) in enumerate(units):
                    st = stage[n % NST]
                    dve.wait_ge(staged[n % NST], 16 * (n // NST + 1))
                    if g is not None:
                        for c in range(C):
                            for k in range(2):
                                chain(dve.tensor_tensor_reduce(
                                    out=junk[:], in0=st[:, c, :], in1=avec[g][:, k, :], scale=1.0 - 2.0 * k,
                                    scalar=0.0, op0=ALU.mult, op1=ALU.add, accum_out=wcol[:, n, c, k:k + 1]))
                        chain(dve.tensor_copy(dst[:, 0, :, D:WC], wcol[:, n, :, :]))
                        chain(dve.tensor_tensor(dst[:, 1, :, D:WC], wcol[:, n, :, :], f(dst[:, 0, :, D:WC]),
                                                ALU.subtract))
                    dve.wait_ge(split_hi, n + 1)
                    dve.tensor_tensor(dst[:, 1, :, 0:D], st[:], f(dst[:, 0, :, 0:D]), ALU.subtract)\
                        .then_inc(split_lo, 1)
                dve.wait_ge(split_lo, NU)
                dve.wait_ge(adj_in, 32)
                chain(dve.tensor_copy(adj_f[:], adj_i[:].bitcast(I32)))
                chain(dve.tensor_copy(adjt_f[:], adjt_i[:].bitcast(I32)))
                chain(dve.tensor_copy(at[:, 0], adjt_f[:]))
                chain(dve.tensor_tensor(at[:, 1], adjt_f[:], f(at[:, 0]), ALU.subtract))
                chain(dve.tensor_scalar(maskp[:], adj_f[:], 0.0, BIG, ALU.is_equal, ALU.mult))
                chain(dve.tensor_scalar(mask3p[:], adj_f[:], 0.0, BIG, ALU.is_le, ALU.mult))
                chain(dve.tensor_reduce(out=deg[:], in_=adj_f[:], axis=AX.X, op=ALU.add))
                chain(dve.tensor_scalar(e2[0][:], adj_f[:], 0.0, None, ALU.not_equal))
                chain(dve.tensor_reduce(out=has[:], in_=e2[0][:], axis=AX.X, op=ALU.max))
                chain(dve.reciprocal(zz[0][:], has[:]))
                chain(dve.tensor_tensor(zz[0][:], zz[0][:], has[:], ALU.mult))
                for c in reversed(range(C)):
                    chain(dve.tensor_scalar(degb[:, c, :], degb[:, 0, :], deg[:, c:c + 1], None, ALU.mult))
                    chain(dve.tensor_scalar(bo_nan[:, c, :], bo_nan[:, 0, :], zz[0][:, c:c + 1], None, ALU.mult))

        rows_ready, rows_T, rows_hi, rows_lo = (sem2(n) for n in ("rows_ready", "rows_T", "rows_hi", "rows_lo"))
        TR_CTX, TR_OUT = 3, 5
        LN_TR = (0, 1, 2, 4)
        var_ready, rstd_ready = sem2("var_ready"), sem2("rstd_ready")
        xb_ready = sem2("xb_ready")
        xb_ok = sem2("xb_ok")
        mj_done, mi_done, mj_hi, mj_lo, amj_done = (sem2(n) for n in ("mj_done", "mi_done", "mj_hi", "mj_lo", "amj_done"))
        wh_done, wh_hi, wh_lo = sem2("wh_done"), sem2("wh_hi"), sem2("wh_lo")
        dbc_done, bias_ready, exp_done = sem2("dbc_done"), sem2("bias_ready"), sem2("exp_done")
        max_done, prob_ready = sem2("max_done"), sem2("prob_ready")
        pT_done, pT_hi, pT_lo, pv_done = sem2("pT_done"), sem2("pT_hi"), sem2("pT_lo"), sem2("pv_done")
        elu_exp, elu_done, hid_hi, hid_lo = (sem2(n) for n in ("elu_exp", "elu_done", "hid_hi", "hid_lo"))
        elu_relu = sem2("elu_relu")
        qkv_done = sem2("qkv_done")
        q_full, q_hi, q_lo = sem2("q_full"), sem2("q_hi"), sem2("q_lo")
        k_full, k_hi, k_lo = sem2("k_full"), sem2("k_hi"), sem2("k_lo")
        v_full, v_a, v_r = sem2("v_full"), sem2("v_a"), sem2("v_r")
        v_b, v_c = sem2("v_b"), sem2("v_c")
        s_done, min_ready, p_done, p_hi, p_lo = (sem2(n) for n in ("s_done", "min_ready", "p_done", "p_hi", "p_lo"))
        p16_done, pT16_ready, o_done, o_used = (sem2(n) for n in ("p16_done", "pT16_ready", "o_done", "o_used"))
        wo_done = sem2("wo_done")
        f1_done, f1_full, f1_hi, f1_lo, f2_done = (sem2(n) for n in ("f1_done", "f1_full", "f1_hi", "f1_lo", "f2_done"))
        ob_ready, x_final = sem2("ob_ready"), sem2("x_final")
        loaded = sem("loaded")
        vstep = sem("vstep")
        sems += [loaded, vstep]
        nums = sorted(q.num for q in sems)
        assert nums == list(range(nums[0], nums[-1] + 1))

        with nc.Fori(0, LOOPS) as i:
            with nc.Block(no_gpsimd_drain=True) as block:

                @block.sync
                def _(sp):
                    for s in S2:
                        sp.wait_ge(rows_ready[s], 1)
                        sp.wait_ge(xb_ready[s], 1)
                        nxt = sp.snap((i * 2 + 2 + s) % B)
                        sp.dma_start(xin[s][:], x[nxt].rearrange("(c p) d -> p c d", p=P)).then_inc(loaded, 16)
                    for s in S2:
                        sp.wait_ge(x_final[s], 1)
                        cur = sp.snap(i * 2 + s)
                        sp.dma_start(out[cur].rearrange("(c p) d -> p c d", p=P), xs[s][:]).then_inc(stored, 16)
                    sp.wait_ge(loaded, 32)

                @block.gpsimd
                def _(pool):
                    def inv_std(k):
                        for s in S2:
                            pool.wait_ge(var_ready[s], k + 1)
                            pool.tensor_tensor(rstd[s][:], ve[s][:], pow_half[:], ALU.pow).then_inc(rstd_ready[s], 1)

                    def scale_probs(g):
                        for s in S2:
                            pool.wait_ge(max_done[s], g + 1)
                            for c in range(C):
                                last = pool.tensor_scalar(pr[s][:, c, :], pr[s][:, c, :], rs[s][:, c:c + 1],
                                                          has[:, c:c + 1] if g == 0 else 1.0, ALU.mult, ALU.mult)
                            last.then_inc(prob_ready[s], 1)

                    inv_std(0)
                    for s in S2:
                        pool.tensor_tensor(e2[s][:], xin[s][:], degb[:], ALU.add).then_inc(xb_ready[s], 1)
                    inv_std(1)
                    scale_probs(0)
                    inv_std(2)
                    for s in S2:
                        pool.wait_ge(q_hi[s], 1)
                        pool.tensor_tensor(hid[s][:, 1, 0:C, :], fu[s][:], f(hid[s][:, 0, 0:C, :]), ALU.subtract)\
                            .then_inc(q_lo[s], 1)
                        pool.wait_ge(k_hi[s], 1)
                        pool.tensor_tensor(hid[s][:, 1, C:2 * C, :], rb[s][:], f(hid[s][:, 0, C:2 * C, :]),
                                           ALU.subtract).then_inc(k_lo[s], 1)
                    for s in S2:
                        pool.wait_ge(v_a[s], 1)
                        pool.tensor_tensor(e2[s][:], e1[s][:], v_part(s, 0), ALU.subtract).then_inc(v_r[s], 1)
                    for s in S2:
                        pool.wait_ge(v_b[s], 1)
                        pool.tensor_tensor(v_part(s, 2), as_heads(e2[s]), v_part(s, 1), ALU.subtract)\
                            .then_inc(v_c[s], 1)
                    for s in S2:
                        pool.wait_ge(xb_ok[s], 1)
                        pool.tensor_tensor(xs[s][:], xs[s][:], bo_nan[:], ALU.add).then_inc(xb_ready[s], 1)
                    for h in range(HQ):
                        for s in S2:
                            pool.wait_ge(p_hi[s], h + 1)
                            pool.tensor_tensor(p16[s][h % 2][:, 1], l2_probs(s, h)[:], p16[s][h % 2][:, 0],
                                               ALU.subtract).then_inc(p_lo[s], 1)
                    inv_std(3)
                    for s in S2:
                        pool.wait_ge(xb_ok[s], 2)
                        for c in range(C):
                            last = pool.tensor_tensor(xs[s][:, c, :], xs[s][:, c, :], beta_b[:], ALU.add)
                        last.then_inc(xb_ready[s], 1)
                    for k in range(HG + 1):
                        if k < HG:
                            scale_probs(1 + k)
                        if k >= 1:
                            for s in S2:
                                pool.wait_ge(hid_hi[s], k)
                                c0 = C * (k - 1)
                                pool.tensor_tensor(hid[s][:, 1, c0:c0 + C, :], fu[s][:],
                                                   f(hid[s][:, 0, c0:c0 + C, :]), ALU.subtract)\
                                    .then_inc(hid_lo[s], 1)
                    scale_probs(GOUT)
                    for s in S2:
                        pool.wait_ge(rows_T[s], TR_OUT + 1)
                        for c in range(C):
                            last = pool.tensor_tensor(fu[s][:, c, :], fu[s][:, c, :], b2_b[:], ALU.add)
                        last.then_inc(ob_ready[s], 1)
                    inv_std(4)

                @block.scalar
                def _(act):
                    def transposed_hi(t, relu):
                        for s in S2:
                            act.wait_ge(rows_T[s], t + 1)
                            k = BD if t == TR_OUT else BC
                            act.activation(hT[s][:, 0], bank(s, k), ACT.Relu if relu else ACT.Copy)\
                                .then_inc(rows_hi[s], 1)

                    def weights_hi(g):
                        for s in S2:
                            act.wait_ge(wh_done[s], g + 1)
                            if g >= 2:
                                act.wait_ge(pv_done[s], g - 1)
                            act.activation(whs[s][g % 2][:, 0], wh_banks(s)[:, :, 0:D], ACT.Copy)\
                                .then_inc(wh_hi[s], 1)

                    def exps(g):
                        for s in S2:
                            act.wait_ge(bias_ready[s], g + 1)
                            if g:
                                act.wait_ge(max_done[s], g)
                            for c in range(C):
                                act.activation(e1[s][:, c, :], tb[s][:, c, :], ACT.Exp,
                                               bias=bias1[s][:, c:c + 1], scale=-1.0)
                                last = act.activation(e2[s][:, c, :], tb[s][:, c, :], ACT.Exp,
                                                      bias=bias2[s][:, c:c + 1], scale=-SLOPE[g])
                            last.then_inc(exp_done[s], 1)

                    def probs_hi(g):
                        for s in S2:
                            act.wait_ge(pT_done[s], g + 1)
                            if g:
                                act.wait_ge(pv_done[s], g)
                            act.activation(pT[s][:, 0], bank(s, BD), ACT.Copy).then_inc(pT_hi[s], 1)

                    def elu_branch(g):
                        src = BD if g < GOUT else BC
                        for s in S2:
                            act.wait_ge(pv_done[s], g + 1)
                            if g >= 2:
                                act.wait_ge(elu_done[s], g - 1)
                            act.activation(rb[s][:], bank(s, src), ACT.Relu, scale=-1.0).then_inc(elu_relu[s], 1)
                        for s in S2:
                            act.wait_ge(elu_relu[s], g)
                            act.activation(rb[s][:], rb[s][:], ACT.Exp, scale=-1.0).then_inc(elu_exp[s], 1)

                    transposed_hi(0, True)
                    for s in S2:
                        act.wait_ge(mj_done[s], 1)
                        act.activation(whs[s][1][:, 0], bank(s, BA), ACT.Copy).then_inc(mj_hi[s], 1)
                    transposed_hi(1, True)
                    weights_hi(0)
                    exps(0)
                    probs_hi(0)
                    transposed_hi(2, True)
                    for s in S2:
                        act.wait_ge(q_full[s], 1)
                        act.activation(hid[s][:, 0, 0:C, :], fu[s][:], ACT.Copy).then_inc(q_hi[s], 1)
                        act.wait_ge(qkv_done[s], 2)
                        for c in range(C):
                            act.activation(rb[s][:, c, :], bank(s, BB)[:, c, :], ACT.Identity,
                                           bias=bk_c[:, c:c + 1]).then_inc(k_full[s], 1)
                        act.wait_ge(k_full[s], C)
                        act.activation(hid[s][:, 0, C:2 * C, :], rb[s][:], ACT.Copy).then_inc(k_hi[s], 1)
                    for s in S2:
                        act.wait_ge(v_full[s], 1)
                        act.activation(v_part(s, 0), as_heads(e1[s]), ACT.Copy).then_inc(v_a[s], 1)
                    for s in S2:
                        act.wait_ge(v_r[s], 1)
                        act.activation(v_part(s, 1), as_heads(e2[s]), ACT.Copy).then_inc(v_b[s], 1)
                    for h in range(HQ):
                        for s in S2:
                            act.wait_ge(min_ready[s], h + 1)
                            if h == 1:
                                act.wait_ge(v_c[s], 1)
                            if h >= 2:
                                act.wait_ge(p_lo[s], h - 1)
                            for c in range(C):
                                last = act.activation(l2_probs(s, h)[:, c, :], l2_logits(s, h)[:, c, :], ACT.Exp,
                                                      bias=hmin[s][h % 2][:, c:c + 1], scale=-1.0)
                            last.then_inc(p_done[s], 1)
                        for s in S2:
                            act.wait_ge(p_done[s], h + 1)
                            if h >= 2:
                                act.wait_ge(p16_done[s], h - 1)
                            act.activation(p16[s][h % 2][:, 0], l2_probs(s, h)[:], ACT.Copy).then_inc(p_hi[s], 1)
                    transposed_hi(TR_CTX, False)
                    transposed_hi(4, True)
                    for k in range(HG + 1):
                        if k < HG:
                            weights_hi(1 + k)
                        if k >= 1:
                            probs_hi(k)
                            elu_branch(k)
                        if k < HG:
                            exps(1 + k)
                        if k >= 1:
                            for s in S2:
                                act.wait_ge(elu_done[s], k)
                                act.activation(hid[s][:, 0, C * (k - 1):C * k, :], fu[s][:], ACT.Copy)\
                                    .then_inc(hid_hi[s], 1)
                    weights_hi(GOUT)
                    exps(GOUT)
                    probs_hi(GOUT)
                    elu_branch(GOUT)
                    transposed_hi(TR_OUT, False)
                    for s in S2:
                        act.wait_ge(f1_done[s], 1)
                        for c in range(C):
                            act.activation(rb[s][:, c, :], bank(s, BA)[:, c, :], ACT.Relu,
                                           bias=b1_c[:, c:c + 1]).then_inc(f1_full[s], 1)
                    for s in S2:
                        act.wait_ge(f1_full[s], C)
                        act.activation(hid[s][:, 0, 0:C, :], rb[s][:], ACT.Copy).then_inc(f1_hi[s], 1)

                @block.tensor
                def _(pe):
                    def product(dst, lhs, rhs, terms):
                        n = 0
                        for t in range(terms):
                            for a, b in PARTS:
                                last = pe.matmul(dst, lhs(a, t), rhs(b, t), start=(n == 0),
                                                 stop=(n == 3 * terms - 1))
                                n += 1
                        return last

                    def blk(k):
                        return slice(k * P, (k + 1) * P)

                    def rows_from(s, k, w):
                        for c in range(C):
                            last = product(bank(s, k)[:, c, :], lambda a, t: hT[s][:, a, t, blk(c)],
                                           lambda b, t: w[:, b, t, :], C)
                        return last

                    def transpose_rows(t):
                        k = BD if t == TR_OUT else BC
                        src = pr if t in LN_TR else fu
                        for s in S2:
                            pe.wait_ge(rows_ready[s], t + 1)
                            for kc in range(C):
                                for c in range(C):
                                    last = pe.transpose(bank(s, k)[:, kc, blk(c)], src[s][:, c, blk(kc)], ident[:])
                            last.then_inc(rows_T[s], 1)

                    def attention_weights(g):
                        for s in S2:
                            if g in (0, 1):
                                pe.wait_ge(rows_lo[s], LN_TR[3 if g else 1] + 1)
                            else:
                                pe.wait_ge(wh_lo[s], g)
                            if g == GOUT:
                                pe.wait_ge(hid_lo[s], HG)
                            for c in range(C):
                                if g == GOUT:
                                    last = product(wh_banks(s)[:, c, 0:WC], lambda a, t: hid[s][:, a, t, blk(c)],
                                                   lambda b, t: wout[:, b, t, :], HG * C)
                                else:
                                    w = w1g[:, :, :, :] if g == 0 else wh[:, :, C * (g - 1):C * g, :]
                                    last = product(wh_banks(s)[:, c, 0:WC], lambda a, t: hT[s][:, a, t, blk(c)],
                                                   lambda b, t: w[:, b, t, :], C)
                            last.then_inc(wh_done[s], 1)

                    def spread_targets(g):
                        for s in S2:
                            pe.wait_ge(wh_lo[s], g + 1)
                            if g >= 2:
                                pe.wait_ge(bias_ready[s], g)
                            for c in range(C):
                                last = pe.matmul(bank(s, BC)[:, 0, blk(c)], cols[s][:, c, 1:2].broadcast_to([P, P]),
                                                 ident[:], start=True, stop=True)
                            last.then_inc(dbc_done[s], 1)

                    def transpose_probs(g):
                        for s in S2:
                            pe.wait_ge(prob_ready[s], g + 1)
                            if g >= 2:
                                pe.wait_ge(elu_done[s], g - 1)
                            for jc in range(C):
                                for c in range(C):
                                    last = pe.transpose(bank(s, BD)[:, jc, blk(c)], pr[s][:, c, blk(jc)], ident[:])
                            last.then_inc(pT_done[s], 1)

                    def attend(g):
                        for s in S2:
                            pe.wait_ge(pT_lo[s], g + 1)
                            w = whs[s][g % 2]
                            for c in range(C):
                                if 1 <= g <= HG:
                                    last = product(bank(s, BD)[:, c, :], lambda a, t: w[:, a, t, blk(c)],
                                                   lambda b, t: pT[s][:, b, t, :], C)
                                else:
                                    last = product(bank(s, BC)[:, c, :], lambda a, t: pT[s][:, a, t, blk(c)],
                                                   lambda b, t: w[:, b, t, :], C)
                            last.then_inc(pv_done[s], 1)

                    transpose_rows(0)
                    for s in S2:
                        pe.wait_ge(rows_lo[s], 1)
                        rows_from(s, BA, w0[:, :, C:2 * C, :]).then_inc(mj_done[s], 1)
                        rows_from(s, BB, w0[:, :, 0:C, :]).then_inc(mi_done[s], 1)
                    for s in S2:
                        pe.wait_ge(mj_lo[s], 1)
                        for c in range(C):
                            last = product(bank(s, BD)[:, c, :], lambda a, t: at[:, a, t, blk(c)],
                                           lambda b, t: whs[s][1][:, b, t, :], C)
                        last.then_inc(amj_done[s], 1)
                    transpose_rows(1)
                    attention_weights(0)
                    spread_targets(0)
                    transpose_probs(0)
                    attend(0)
                    transpose_rows(2)
                    for s in S2:
                        pe.wait_ge(rows_lo[s], 3)
                        for k, w in ((BA, wq), (BB, wk)):
                            for c in range(C):
                                last = product(bank(s, k)[:, c, :], lambda a, t: w[:, a, t, blk(c)],
                                               lambda b, t: hT[s][:, b, t, :], C)
                            last.then_inc(qkv_done[s], 1)
                        rows_from(s, BC, wv).then_inc(qkv_done[s], 1)
                    for k in range(HQ + 2):
                        if k < HQ:
                            r = slice(DH * (k % 4), DH * (k % 4) + DH)
                            oc = k // 4
                            for s in S2:
                                if k == 0:
                                    pe.wait_ge(q_lo[s], 1)
                                    pe.wait_ge(k_lo[s], 1)
                                if k >= 2:
                                    pe.wait_ge(min_ready[s], k - 1)
                                for c in range(C):
                                    for n, (a, b) in enumerate(PARTS):
                                        last = pe.matmul(bank(s, k % 2)[:, c, :], hid[s][r, a, oc, blk(c)],
                                                         hid[s][r, b, C + oc, :], start=(n == 0), stop=(n == 2))
                                last.then_inc(s_done[s], 1)
                        if k >= 2:
                            h = k - 2
                            for s in S2:
                                pe.wait_ge(pT16_ready[s], h + 1)
                                if h == 0:
                                    pe.wait_ge(v_c[s], 1)
                                if h % 2 == 0 and h:
                                    pe.wait_ge(o_used[s], h // 2)
                                for c in range(C):
                                    dst = ps[s][:, BD * BANK + ((h % 2) * C + c) * VC:
                                                BD * BANK + ((h % 2) * C + c + 1) * VC]
                                    n = 0
                                    for part in range(2):
                                        for kc in range(C):
                                            last = pe.matmul(dst, pT16[s][:, part, kc, blk(c)], v3[s][:, kc, h, :],
                                                             start=(n == 0), stop=(n == 2 * C - 1))
                                            n += 1
                                last.then_inc(o_done[s], 1)
                        if 1 <= k <= HQ:
                            h = k - 1
                            for s in S2:
                                pe.wait_ge(p_lo[s], h + 1)
                                if h == 0:
                                    pe.wait_ge(v_full[s], 1)
                                else:
                                    pe.wait_ge(pT16_ready[s], h)
                                for part in range(2):
                                    for kc in range(C):
                                        for c in range(C):
                                            last = pe.transpose(bank16(s, BC)[:, part, kc, blk(c)],
                                                                p16[s][h % 2][:, part, c, blk(kc)], ident16[:])
                                last.then_inc(p16_done[s], 1)
                    transpose_rows(TR_CTX)
                    for s in S2:
                        pe.wait_ge(rows_lo[s], TR_CTX + 1)
                        rows_from(s, BA, wo).then_inc(wo_done[s], 1)
                    transpose_rows(4)
                    for k in range(HG + 1):
                        if k < HG:
                            attention_weights(1 + k)
                        if k >= 1:
                            transpose_probs(k)
                        if k < HG:
                            spread_targets(1 + k)
                        if k >= 1:
                            attend(k)
                    attention_weights(GOUT)
                    spread_targets(GOUT)
                    transpose_probs(GOUT)
                    attend(GOUT)
                    transpose_rows(TR_OUT)
                    for s in S2:
                        pe.wait_ge(rows_lo[s], TR_OUT + 1)
                        for c in range(C):
                            last = product(bank(s, BA)[:, c, :], lambda a, t: wf1[:, a, t, blk(c)],
                                           lambda b, t: hT[s][:, b, t, :], C)
                        last.then_inc(f1_done[s], 1)
                    for s in S2:
                        pe.wait_ge(f1_lo[s], 1)
                        for c in range(C):
                            last = product(bank(s, BB)[:, c, :], lambda a, t: hid[s][:, a, t, blk(c)],
                                           lambda b, t: wf2[:, b, t, :], C)
                        last.then_inc(f2_done[s], 1)

                @block.vector
                def _(dve):
                    steps = [0]

                    def mark(ins):
                        steps[0] += 1
                        ins.then_inc(vstep, 1)
                        return steps[0]

                    def after(n):
                        dve.wait_ge(vstep, n)

                    def norm_stats(src):
                        a = [[mark(dve.bn_stats(stats[s][:, c, :], src[s][:, c, :])) for c in range(C)] for s in S2]
                        b = []
                        for s in S2:
                            after(a[s][-1])
                            b.append([mark(dve.bn_aggr(mv[s][:, c, :], stats[s][:, c, :])) for c in range(C)])
                        for s in S2:
                            after(b[s][-1])
                            dve.tensor_scalar(ve[s][:], mv[s][:, :, 1], EPS, None, ALU.add).then_inc(var_ready[s], 1)

                    def norm_rows(k, src, t):
                        for s in S2:
                            dve.wait_ge(rstd_ready[s], k + 1)
                            for c in range(C):
                                last = dve.tensor_scalar(pr[s][:, c, :], src[s][:, c, :], mv[s][:, c, 0:1],
                                                         rstd[s][:, c:c + 1], ALU.subtract, ALU.mult)
                            last.then_inc(rows_ready[s], 1)

                    def transposed_lo(t, relu):
                        for s in S2:
                            dve.wait_ge(rows_hi[s], t + 1)
                            src = bank(s, BD if t == TR_OUT else BC)
                            dst, hi = hT[s][:, 1], f(hT[s][:, 0])
                            if relu:
                                ins = dve.scalar_tensor_tensor(out=dst, in0=src, scalar=0.0, in1=hi,
                                                               op0=ALU.max, op1=ALU.subtract)
                            else:
                                ins = dve.tensor_tensor(dst, src, hi, ALU.subtract)
                            ins.then_inc(rows_lo[s], 1)

                    def weights_lo(g):
                        for s in S2:
                            dve.wait_ge(wh_hi[s], g + 1)
                            mark(dve.tensor_copy(cols[s][:], wh_banks(s)[:, :, D:WC]))
                            dve.tensor_tensor(whs[s][g % 2][:, 1], wh_banks(s)[:, :, 0:D],
                                              f(whs[s][g % 2][:, 0]), ALU.subtract).then_inc(wh_lo[s], 1)

                    def row_maxima(g):
                        m = maskp if g == 0 else mask3p
                        n = []
                        for s in S2:
                            dve.wait_ge(dbc_done[s], g + 1)
                            if g:
                                dve.wait_ge(exp_done[s], g)
                            for c in range(C):
                                last = dve.tensor_tensor_reduce(
                                    out=tb[s][:, c, :], in0=bank(s, BC)[:, 0, :], in1=m[:, c, :], scale=1.0,
                                    scalar=3.0e38, op0=ALU.add, op1=ALU.min, accum_out=dmin[s][:, c:c + 1])
                            n.append(mark(last))
                        for s in S2:
                            after(n[s])
                            n[s] = mark(dve.tensor_tensor(zz[s][:], cols[s][:, :, 0], dmin[s][:], ALU.subtract))
                        for s in S2:
                            after(n[s])
                            n[s] = mark(dve.scalar_tensor_tensor(out=mm[s][:], in0=zz[s][:], scalar=SLOPE[g],
                                                                 in1=zz[s][:], op0=ALU.mult, op1=ALU.max))
                        for s in S2:
                            after(n[s])
                            mark(dve.tensor_tensor(bias1[s][:], cols[s][:, :, 0], mm[s][:], ALU.subtract))
                            dve.scalar_tensor_tensor(out=bias2[s][:], in0=cols[s][:, :, 0], scalar=SLOPE[g],
                                                     in1=mm[s][:], op0=ALU.mult, op1=ALU.subtract)\
                                .then_inc(bias_ready[s], 1)

                    def leaky_probs(g):
                        n = []
                        for s in S2:
                            dve.wait_ge(exp_done[s], g + 1)
                            if g:
                                dve.wait_ge(pT_done[s], g)
                            for c in range(C):
                                last = dve.scalar_tensor_tensor(out=pr[s][:, c, :], in0=e1[s][:, c, :], scalar=1.0,
                                                                in1=e2[s][:, c, :], op0=ALU.mult, op1=ALU.max,
                                                                accum_out=psums[s][:, c:c + 1])
                            n.append(mark(last))
                        for s in S2:
                            after(n[s])
                            dve.reciprocal(rs[s][:], psums[s][:]).then_inc(max_done[s], 1)

                    def probs_lo(g):
                        for s in S2:
                            dve.wait_ge(pT_hi[s], g + 1)
                            dve.tensor_tensor(pT[s][:, 1], bank(s, BD), f(pT[s][:, 0]), ALU.subtract)\
                                .then_inc(pT_lo[s], 1)

                    def elu(g):
                        for s in S2:
                            dve.wait_ge(elu_exp[s], g)
                            if 2 <= g:
                                dve.wait_ge(hid_lo[s], g - 1)
                            ins = dve.scalar_tensor_tensor(out=fu[s][:], in0=rb[s][:], scalar=-1.0,
                                                           in1=bank(s, BD if g < GOUT else BC), op0=ALU.add,
                                                           op1=ALU.max)
                            ins.then_inc(elu_done[s] if g < GOUT else rows_ready[s], 1)

                    norm_stats(xin)
                    norm_rows(0, xin, 0)
                    transposed_lo(0, True)
                    for s in S2:
                        dve.wait_ge(mj_hi[s], 1)
                        dve.tensor_tensor(whs[s][1][:, 1], bank(s, BA), f(whs[s][1][:, 0]), ALU.subtract)\
                            .then_inc(mj_lo[s], 1)
                    dve.wait_ge(stored, dve.snap(i * 32 + 32))
                    n = []
                    for s in S2:
                        dve.wait_ge(mi_done[s], 1)
                        dve.wait_ge(xb_ready[s], 1)
                        for c in range(C):
                            last = dve.scalar_tensor_tensor(out=xs[s][:, c, :], in0=bank(s, BB)[:, c, :],
                                                            scalar=deg[:, c:c + 1], in1=e2[s][:, c, :],
                                                            op0=ALU.mult, op1=ALU.add)
                        n.append(mark(last))
                    for s in S2:
                        dve.wait_ge(amj_done[s], 1)
                        after(n[s])
                        n[s] = mark(dve.tensor_tensor(xs[s][:], xs[s][:], bank(s, BD), ALU.add))
                    after(n[-1])
                    norm_stats(xs)
                    norm_rows(1, xs, 1)
                    transposed_lo(1, True)
                    weights_lo(0)
                    row_maxima(0)
                    leaky_probs(0)
                    probs_lo(0)
                    for s in S2:
                        dve.wait_ge(pv_done[s], 1)
                        n[s] = mark(dve.tensor_tensor(xs[s][:], xs[s][:], bank(s, BC), ALU.add))
                    after(n[-1])
                    norm_stats(xs)
                    norm_rows(2, xs, 2)
                    for s in S2:
                        dve.wait_ge(rows_ready[s], 3)
                        dve.sem_inc(xb_ok[s], 1)
                    transposed_lo(2, True)
                    for s in S2:
                        dve.wait_ge(qkv_done[s], 1)
                        for c in range(C):
                            last = dve.tensor_scalar(fu[s][:, c, :], bank(s, BA)[:, c, :], bq_c[:, c:c + 1], -SCALE,
                                                     ALU.add, ALU.mult)
                        last.then_inc(q_full[s], 1)
                        dve.wait_ge(qkv_done[s], 3)
                        for c in range(C):
                            last = dve.tensor_tensor(e1[s][:, c, :], bank(s, BC)[:, c, :], bv_b[:], ALU.add)
                        last.then_inc(v_full[s], 1)
                    for k in range(HQ + 2):
                        if k < HQ:
                            for s in S2:
                                dve.wait_ge(s_done[s], k + 1)
                                if k == 1:
                                    dve.wait_ge(v_c[s], 1)
                                if k >= 2:
                                    dve.wait_ge(p_done[s], k - 1)
                                for c in range(C):
                                    last = dve.tensor_tensor_reduce(
                                        out=l2_logits(s, k)[:, c, :], in0=bank(s, k % 2)[:, c, :],
                                        in1=maskp[:, c, :], scale=1.0, scalar=3.0e38, op0=ALU.add, op1=ALU.min,
                                        accum_out=hmin[s][k % 2][:, c:c + 1])
                                last.then_inc(min_ready[s], 1)
                        if k >= 2 and k % 2 == 1:
                            h = k - 3
                            for s in S2:
                                dve.wait_ge(o_done[s], h + 2)
                                o = ps[s][:, BD * BANK:BD * BANK + 2 * C * VC].rearrange("p (g v) -> p g v", v=VC)
                                dst = fu[s][:, :, h * DH:(h + 2) * DH].rearrange("p c (h d) -> p h c d", h=2)
                                mark(dve.reciprocal(rden[s][:], o[:, :, 3 * DH]))
                                for hh in range(2):
                                    last = dve.tensor_reduce(
                                        out=dst[:, hh], axis=AX.X, op=ALU.add,
                                        in_=o[:, hh * C:hh * C + C, 0:3 * DH].rearrange("p c (t d) -> p c d t", t=3))
                                last.then_inc(o_used[s], 1)
                            for s in S2:
                                dve.wait_ge(o_used[s], h // 2 + 1)
                                dst = fu[s][:, :, h * DH:(h + 2) * DH].rearrange("p c (h d) -> p h c d", h=2)
                                for hh in range(2):
                                    r = rden[s][:, hh * C:hh * C + C].rearrange("p (c o) -> p c o", o=1)
                                    last = dve.tensor_tensor(dst[:, hh], dst[:, hh],
                                                             r.broadcast_to([P, C, DH]), ALU.mult)
                                if h + 2 == HQ:
                                    last.then_inc(rows_ready[s], 1)
                                else:
                                    mark(last)
                        if 1 <= k <= HQ:
                            h = k - 1
                            for s in S2:
                                dve.wait_ge(p16_done[s], h + 1)
                                if h:
                                    dve.wait_ge(o_done[s], h)
                                dve.tensor_copy(pT16[s][:], bank16(s, BC)).then_inc(pT16_ready[s], 1)
                    transposed_lo(TR_CTX, False)
                    for s in S2:
                        dve.wait_ge(wo_done[s], 1)
                        dve.wait_ge(xb_ready[s], 2)
                        n[s] = mark(dve.tensor_tensor(xs[s][:], xs[s][:], bank(s, BA), ALU.add))
                    after(n[-1])
                    norm_stats(xs)
                    norm_rows(3, xs, 4)
                    for s in S2:
                        dve.wait_ge(rows_ready[s], 5)
                        dve.sem_inc(xb_ok[s], 1)
                    transposed_lo(4, True)
                    for k in range(HG + 1):
                        if k < HG:
                            weights_lo(1 + k)
                        if k >= 1:
                            probs_lo(k)
                        if k < HG:
                            row_maxima(1 + k)
                        if k >= 1:
                            elu(k)
                        if k < HG:
                            leaky_probs(1 + k)
                    weights_lo(GOUT)
                    row_maxima(GOUT)
                    leaky_probs(GOUT)
                    probs_lo(GOUT)
                    elu(GOUT)
                    transposed_lo(TR_OUT, False)
                    for s in S2:
                        dve.wait_ge(f1_hi[s], 1)
                        dve.tensor_tensor(hid[s][:, 1, 0:C, :], rb[s][:], f(hid[s][:, 0, 0:C, :]), ALU.subtract)\
                            .then_inc(f1_lo[s], 1)
                    for s in S2:
                        dve.wait_ge(f2_done[s], 1)
                        dve.wait_ge(ob_ready[s], 1)
                        n[s] = mark(dve.tensor_tensor(e1[s][:], fu[s][:], bank(s, BB), ALU.add))
                    after(n[-1])
                    norm_stats(e1)
                    for s in S2:
                        for c in range(C):
                            last = dve.scalar_tensor_tensor(out=e2[s][:, c, :], in0=e1[s][:, c, :],
                                                            scalar=mv[s][:, c, 0:1], in1=gamma_b[:],
                                                            op0=ALU.subtract, op1=ALU.mult)
                        n[s] = mark(last)
                    for s in S2:
                        after(n[s])
                        dve.wait_ge(rstd_ready[s], 5)
                        dve.wait_ge(xb_ready[s], 3)
                        for c in range(C):
                            last = dve.scalar_tensor_tensor(out=xs[s][:, c, :], in0=e2[s][:, c, :],
                                                            scalar=rstd[s][:, c:c + 1], in1=xs[s][:, c, :],
                                                            op0=ALU.mult, op1=ALU.add)
                        last.then_inc(x_final[s], 1)

            nc.all_engine_barrier(sems_to_clear=range(nums[0], nums[-1] + 1))

        with nc.Block() as block:
            @block.sync
            def _(sp):
                sp.wait_ge(stored, 32 * LOOPS + 32)


def kernel(**inputs):
    import numpy as np
    import concourse.bacc as bacc
    from concourse import mybir as _mybir
    from concourse.bass_utils import run_bass_kernel_spmd

    def t(a):
        return np.ascontiguousarray(np.asarray(a).T)

    g = {k: np.ascontiguousarray(np.asarray(v)) for k, v in inputs.items()}
    arrays = {
        "x_in": g["x"], "adj": g["adj"], "adj_t": t(g["adj"]),
        "L0_W_t": t(g["L0_gnn_W"]), "L0_b": g["L0_gnn_b"],
        "L1_W": g["L1_gnn_W"], "L1_a_src": g["L1_gnn_a_src"], "L1_a_dst": g["L1_gnn_a_dst"],
        "Wq_t": t(g["L2_gnn_Wq"]), "bq": g["L2_gnn_bq"], "Wk_t": t(g["L2_gnn_Wk"]), "bk": g["L2_gnn_bk"],
        "Wv_t": t(g["L2_gnn_Wv"]), "bv": g["L2_gnn_bv"], "Wo_t": t(g["L2_gnn_Wo"]), "bo": g["L2_gnn_bo"],
        "W_heads": g["L3_gnn_W_heads"], "a_heads": g["L3_gnn_a_heads"], "W_out": g["L3_gnn_W_out"],
        "a_out": g["L3_gnn_a_out"], "w1": g["L3_gnn_w1"], "b1": g["L3_gnn_b1"], "w2": g["L3_gnn_w2"],
        "b2": g["L3_gnn_b2"], "gamma": g["L3_gnn_ln_gamma"], "beta": g["L3_gnn_ln_beta"],
    }
    nc = bacc.Bacc("TRN2", target_bir_lowering=False, num_devices=1)
    args = [nc.dram_tensor(k, a.shape, _mybir.dt.from_np(a.dtype), kind="ExternalInput").ap()
            for k, a in arrays.items()]
    out = nc.dram_tensor("out", g["x"].shape, _mybir.dt.float32, kind="ExternalOutput").ap()
    adj_preln_kernel(nc, *args, out)
    r = run_bass_kernel_spmd(nc, [arrays], core_ids=[0])
    return r.results[0]["out"]
```

```python
import concourse.bass as bass
from concourse import mybir
from contextlib import ExitStack


def adj_preln_kernel(nc, x, adj, adj_t, L0_W_t, L0_b, L1_W, L1_a_src, L1_a_dst,
                     Wq_t, bq, Wk_t, bk, Wv_t, bv, Wo_t, bo,
                     W_heads, a_heads, W_out, a_out, w1, b1, w2, b2, gamma, beta, out):
    F32, F32R = mybir.dt.float32, mybir.dt.float32r
    F16, BF16, I32 = mybir.dt.float16, mybir.dt.bfloat16, mybir.dt.int32
    ALU, ACT, AX = mybir.AluOpType, mybir.ActivationFunctionType, mybir.AxisListType

    B, N, D = x.shape
    P = 128
    C = N // P
    assert N == D == 2 * P and B % 2 == 0
    HQ = 8
    DH = D // HQ
    HG = W_heads.shape[0]
    SCALE = float(DH) ** -0.5
    BIG = 1.0e30
    EPS = 1e-5
    SLOPE = [0.2] + [0.01] * (HG + 1)
    GOUT = HG + 1
    WC = D + 2
    VC = 3 * DH + 1
    S2 = (0, 1)
    BANK = 512
    PARTS = ((0, 0), (0, 1), (1, 0))
    LOOPS = B // 2

    ctx = ExitStack()
    with ctx:
        def sb(name, shape, dt=F32):
            return ctx.enter_context(nc.sbuf_tensor(name, shape, dt))

        def sem(name):
            return ctx.enter_context(nc.semaphore(name))

        sems = []

        def sem2(name):
            pair = [sem(f"{name}{s}") for s in S2]
            sems.extend(pair)
            return pair

        w0 = sb("w0", [P, 2, 2 * C, D], F32R)
        w1g = sb("w1g", [P, 2, C, WC], F32R)
        wq = sb("wq", [P, 2, C, D], F32R)
        wk = sb("wk", [P, 2, C, D], F32R)
        wv = sb("wv", [P, 2, C, D], F32R)
        wo = sb("wo", [P, 2, C, D], F32R)
        wh = sb("wh", [P, 2, HG * C, WC], F32R)
        wout = sb("wout", [P, 2, HG * C, WC], F32R)
        wf1 = sb("wf1", [P, 2, C, D], F32R)
        wf2 = sb("wf2", [P, 2, C, D], F32R)
        at = sb("at", [P, 2, C, N], F32R)
        maskp = sb("maskp", [P, C, N])
        mask3p = sb("mask3p", [P, C, N])
        deg = sb("deg", [P, C])
        has = sb("has", [P, C])
        degb = sb("degb", [P, C, D])
        bo_nan = sb("bo_nan", [P, C, D])
        bv_b = sb("bv_b", [P, D])
        b2_b = sb("b2_b", [P, D])
        gamma_b = sb("gamma_b", [P, D])
        beta_b = sb("beta_b", [P, D])
        bq_c = sb("bq_c", [P, C])
        bk_c = sb("bk_c", [P, C])
        b1_c = sb("b1_c", [P, C])
        ident = sb("ident", [P, P])
        ident16 = sb("ident16", [P, P], F16)
        pow_half = sb("pow_half", [P, C])

        def per(name, shape, dt=F32):
            return [sb(f"{name}_{s}", shape, dt) for s in S2]

        xin = per("xin", [P, C, D])
        xs = per("xs", [P, C, D])
        tb = per("tb", [P, C, N])
        e1 = per("e1", [P, C, N])
        e2 = per("e2", [P, C, N])
        pr = per("pr", [P, C, N])
        rb = per("rb", [P, C, N])
        fu = per("fu", [P, C, N])
        hT = per("hT", [P, 2, C, N], F32R)
        whs = [[sb(f"whs{k}_{s}", [P, 2, C, D], F32R) for k in range(2)] for s in S2]
        pT = per("pT", [P, 2, C, N], F32R)
        hid = per("hid", [P, 2, HG * C, N], F32R)
        v3 = per("v3", [P, C, HQ, VC], BF16)
        p16 = [[sb(f"p16{k}_{s}", [P, 2, C, N], F16) for k in range(2)] for s in S2]
        pT16 = per("pT16", [P, 2, C, N], F16)
        cols = [per(f"cols{k}", [P, C, 2]) for k in range(2)]
        dmin = per("dmin", [P, C])
        zz = per("zz", [P, C])
        mm = per("mm", [P, C])
        bias1 = [per(f"bias1{k}", [P, C]) for k in range(2)]
        bias2 = [per(f"bias2{k}", [P, C]) for k in range(2)]
        psums = per("psums", [P, C])
        rs = [per(f"rs{k}", [P, C]) for k in range(2)]
        hmin = [[sb(f"hmin{k}_{s}", [P, C]) for k in range(2)] for s in S2]
        rden = per("rden", [P, 2 * C])
        stats = per("stats", [P, C, 6])
        mv = per("mv", [P, C, 2])
        ve = per("ve", [P, C])
        rstd = per("rstd", [P, C])

        ps = [ctx.enter_context(nc.psum_tensor(f"ps{s}", [P, 4 * BANK], F32)) for s in S2]
        BA, BB, BC, BD = range(4)

        def bank(s, k, n=N):
            return ps[s][:, k * BANK:k * BANK + 2 * n].rearrange("p (c n) -> p c n", c=2)

        def wh_banks(s):
            return ps[s][:, 0:2 * BANK].rearrange("p (c n) -> p c n", c=2)

        def bank16(s, k):
            return ps[s][:, k * BANK:(k + 1) * BANK].bitcast(F16).rearrange("p (t c n) -> p t c n", t=2, c=C)

        def f(t):
            return t.bitcast(F32)

        def as_heads(t):
            return t[:].rearrange("p c (h d) -> p c h d", h=HQ)

        def v_part(s, k):
            return v3[s][:, :, :, k * DH:(k + 1) * DH]

        def l2_logits(s, h):
            return (tb, e1)[h % 2][s]

        def l2_probs(s, h):
            return (pr, e2)[h % 2][s]

        stored = [sem("stored0"), sem("stored1")]

        stage = [tb[0], e1[0], e2[0], pr[0], rb[0], fu[0], tb[1], e1[1]]
        NST = len(stage)
        avec = [e2[1], pr[1], rb[1], fu[1], xs[0], xs[1]]

        def halves(w, k):
            return w[k * D:(k + 1) * D, :].rearrange("(c p) n -> p c n", p=P)

        units = [(halves(L0_W_t, 0), w0[:, :, 0:C, :], None), (halves(L0_W_t, 1), w0[:, :, C:2 * C, :], None),
                 (halves(L1_W, 0), w1g[:, :, :, :], 0),
                 (halves(Wq_t, 0), wq[:, :, :, :], None), (halves(Wk_t, 0), wk[:, :, :, :], None),
                 (halves(Wv_t, 0), wv[:, :, :, :], None), (halves(Wo_t, 0), wo[:, :, :, :], None)]
        units += [(halves(W_heads[h], 0), wh[:, :, C * h:C * h + C, :], 1 + h) for h in range(HG)]
        units += [(halves(W_out, h), wout[:, :, C * h:C * h + C, :], GOUT) for h in range(HG)]
        units += [(halves(w1, 0), wf1[:, :, :, :], None), (halves(w2, 0), wf2[:, :, :, :], None)]
        avecs = [(L1_a_src, L1_a_dst)] + [(a_heads[h, 0:D], a_heads[h, D:2 * D]) for h in range(HG)] \
            + [(a_out[0:D], a_out[D:2 * D])]
        NU = len(units)

        def bcast(v):
            return v.rearrange("(o n) -> o n", o=1).broadcast_to([P, v.shape[0]])

        def column(v):
            return v.rearrange("(c p) -> p c", p=P)

        staged = [sem(f"staged{k}") for k in range(NST)]
        small = sem("small")
        adj_in = sem("adj_in")
        split_hi = sem("split_hi")
        split_lo = sem("split_lo")
        scored = sem("scored")
        made = sem("made")
        pooled = sem("pooled")
        first_x = sem("first_x")
        wcol = sb("wcol", [P, NU, C, 2])
        junk = sb("junk", [P, D])
        adj_i, adjt_i, adj_f, adjt_f = (hT_alias for hT_alias in (
            xs[0], xs[1], tb[0], e1[0]))

        n_small = 0
        N_MADE = sum(2 * C + 2 for _, _, g in units if g is not None) + 11 + 2 * C
        with nc.Block() as block:
            @block.sync
            def _(sp):
                sp.sem_inc(stored[0], 16)
                for s in S2:
                    sp.dma_start(xin[s][:], x[s].rearrange("(c p) d -> p c d", p=P)).then_inc(first_x, 16)
                for n, (src, _, _) in enumerate(units):
                    if n >= NST:
                        sp.wait_ge(split_lo, n - NST + 1)
                    sp.dma_start(stage[n % NST][:], src).then_inc(staged[n % NST], 16)
                sp.wait_ge(split_lo, NU)
                sp.dma_start(adj_i[:].bitcast(I32), adj.rearrange("(c p) n -> p c n", p=P)).then_inc(adj_in, 16)
                sp.dma_start(adjt_i[:].bitcast(I32), adj_t.rearrange("(c p) n -> p c n", p=P)).then_inc(adj_in, 16)
                sp.wait_ge(made, N_MADE)
                sp.dma_start(xs[1][:], x[1].rearrange("(c p) d -> p c d", p=P)).then_inc(first_x, 16)
                sp.wait_ge(first_x, 48)

            @block.gpsimd
            def _(pool):
                pool.memset(ident[:], 0.0).then_inc(pooled, 1)
                pool.memset(pow_half[:], -0.5).then_inc(pooled, 1)
                for s in S2:
                    pool.memset(v3[s][:], 1.0).then_inc(pooled, 1)
                pool.wait_ge(pooled, 4)
                pool.affine_select(out=ident[:], in_=ident[:], compare_op=ALU.not_equal, fill=1.0, base=0,
                                   pattern=[[-1, P]], channel_multiplier=1).then_inc(pooled, 1)
                pool.wait_ge(pooled, 5)
                pool.tensor_copy(ident16[:], ident[:]).then_inc(pooled, 1)

            @block.scalar
            def _(act):
                for k, (a, b) in enumerate(avecs):
                    act.dma_start(avec[k][:, 0, :], bcast(a)).then_inc(small, 16)
                    act.dma_start(avec[k][:, 1, :], bcast(b)).then_inc(small, 16)
                for dst, v in ((bv_b, bv), (b2_b, b2), (gamma_b, gamma), (beta_b, beta)):
                    act.dma_start(dst[:], bcast(v)).then_inc(small, 16)
                act.dma_start(degb[:, 0, :], bcast(L0_b)).then_inc(small, 16)
                act.dma_start(bo_nan[:, 0, :], bcast(bo)).then_inc(small, 16)
                for dst, v in ((bq_c, bq), (bk_c, bk), (b1_c, b1)):
                    with nc.allow_non_contiguous_dma(reason="bias columns, once"):
                        act.dma_start(dst[:], column(v)).then_inc(small, 16)
                for n, (_, dst, _) in enumerate(units):
                    act.wait_ge(staged[n % NST], 16 * (n // NST + 1))
                    act.activation(dst[:, 0, :, 0:D], stage[n % NST][:], ACT.Copy).then_inc(split_hi, 1)

            @block.vector
            def _(dve):
                step = 0

                def chain(ins):
                    nonlocal step
                    step += 1
                    ins.then_inc(made, 1)
                    dve.wait_ge(made, step)

                dve.wait_ge(small, 16 * (2 * len(avecs) + 9))
                for n, (_, dst, g) in enumerate(units):
                    st = stage[n % NST]
                    dve.wait_ge(staged[n % NST], 16 * (n // NST + 1))
                    if g is not None:
                        for c in range(C):
                            for k in range(2):
                                chain(dve.tensor_tensor_reduce(
                                    out=junk[:], in0=st[:, c, :], in1=avec[g][:, k, :], scale=1.0 - 2.0 * k,
                                    scalar=0.0, op0=ALU.mult, op1=ALU.add, accum_out=wcol[:, n, c, k:k + 1]))
                        chain(dve.tensor_copy(dst[:, 0, :, D:WC], wcol[:, n, :, :]))
                        chain(dve.tensor_tensor(dst[:, 1, :, D:WC], wcol[:, n, :, :], f(dst[:, 0, :, D:WC]),
                                                ALU.subtract))
                    dve.wait_ge(split_hi, n + 1)
                    dve.tensor_tensor(dst[:, 1, :, 0:D], st[:], f(dst[:, 0, :, 0:D]), ALU.subtract)\
                        .then_inc(split_lo, 1)
                dve.wait_ge(split_lo, NU)
                dve.wait_ge(adj_in, 32)
                chain(dve.tensor_copy(adj_f[:], adj_i[:].bitcast(I32)))
                chain(dve.tensor_copy(adjt_f[:], adjt_i[:].bitcast(I32)))
                chain(dve.tensor_copy(at[:, 0], adjt_f[:]))
                chain(dve.tensor_tensor(at[:, 1], adjt_f[:], f(at[:, 0]), ALU.subtract))
                chain(dve.tensor_scalar(maskp[:], adj_f[:], 0.0, BIG, ALU.is_equal, ALU.mult))
                chain(dve.tensor_scalar(mask3p[:], adj_f[:], 0.0, BIG, ALU.is_le, ALU.mult))
                chain(dve.tensor_reduce(out=deg[:], in_=adj_f[:], axis=AX.X, op=ALU.add))
                chain(dve.tensor_scalar(e2[0][:], adj_f[:], 0.0, None, ALU.not_equal))
                chain(dve.tensor_reduce(out=has[:], in_=e2[0][:], axis=AX.X, op=ALU.max))
                chain(dve.reciprocal(zz[0][:], has[:]))
                chain(dve.tensor_tensor(zz[0][:], zz[0][:], has[:], ALU.mult))
                for c in reversed(range(C)):
                    chain(dve.tensor_scalar(degb[:, c, :], degb[:, 0, :], deg[:, c:c + 1], None, ALU.mult))
                    chain(dve.tensor_scalar(bo_nan[:, c, :], bo_nan[:, 0, :], zz[0][:, c:c + 1], None, ALU.mult))
                assert step == N_MADE

        TE, SC, VE, PO = range(4)

        def norm_chain(a, n, t, src):
            a("stats", n, VE, 0.65, src)
            a("aggr", n, VE, 0.15, ("stats", n))
            a("var", n, VE, 0.08, ("aggr", n))
            a("inv_std", n, PO, 0.3, ("var", n))
            a("rows", n, VE, 0.45, ("inv_std", n))
            transposed(a, t, ("rows", n))

        def transposed(a, t, src):
            a("rows_T", t, TE, 0.25, src)
            a("rows_hi", t, SC, 0.6, ("rows_T", t))
            a("rows_lo", t, VE, 0.62, ("rows_hi", t))

        def graph_attention(a, g, src):
            a("wh", g, TE, 5.2 if g == GOUT else 1.35, src, ("wh_lo", g - 1), *(("hid_lo", h) for h in range(1, g) if g == GOUT))
            a("wh_hi", g, SC, 0.6, ("wh", g), ("attend", g - 2))
            a("wh_lo", g, VE, 0.75, ("wh_hi", g), ("biases", g - 2))
            a("spread", g, TE, 0.45, ("wh_lo", g), ("tmin", g - 1))
            a("tmin", g, VE, 0.7, ("spread", g), ("exps", g - 1))
            a("top", g, VE, 0.08, ("tmin", g))
            a("leaky_top", g, VE, 0.08, ("top", g))
            a("biases", g, VE, 0.16, ("leaky_top", g))
            a("exps", g, SC, 1.4, ("biases", g), ("larger", g - 1))
            a("larger", g, VE, 0.75, ("exps", g), ("probs_T", g - 1))
            a("inv_sum", g, VE, 0.08, ("larger", g))
            a("scale", g, PO, 1.1, ("inv_sum", g))
            a("probs_T", g, TE, 0.25, ("scale", g), ("elu", g - 1))
            a("probs_hi", g, SC, 0.6, ("probs_T", g), ("attend", g - 1))
            a("probs_lo", g, VE, 0.62, ("probs_hi", g))
            a("attend", g, TE, 1.3, ("probs_lo", g))
            if g:
                a("elu_relu", g, SC, 0.6, ("attend", g), ("elu", g - 1))
                a("elu_exp", g, SC, 0.6, ("elu_relu", g))
                a("elu", g, VE, 0.62, ("elu_exp", g), ("hid_lo", g - 1))
            if 1 <= g <= HG:
                a("hid_hi", g, SC, 0.6, ("elu", g))
                a("hid_lo", g, PO, 1.2, ("hid_hi", g))

        def front(a):
            a("x_deg", 0, PO, 1.2)
            norm_chain(a, 0, 0, None)
            a("mj", 0, TE, 1.3, ("rows_lo", 0))
            a("mi", 0, TE, 1.3, ("rows_lo", 0))
            a("mj_hi", 0, SC, 0.6, ("mj", 0))
            a("mj_lo", 0, VE, 0.6, ("mj_hi", 0))
            a("x_mi", 0, VE, 0.7, ("mi", 0), ("x_deg", 0))
            a("amj", 0, TE, 1.3, ("mj_lo", 0))
            a("x1", 0, VE, 0.6, ("amj", 0), ("x_mi", 0))
            norm_chain(a, 1, 1, ("x1", 0))
            graph_attention(a, 0, ("rows_lo", 1))
            a("x2", 0, VE, 0.6, ("attend", 0))
            norm_chain(a, 2, 2, ("x2", 0))
            a("q", 0, TE, 1.3, ("rows_lo", 2))
            a("k", 0, TE, 1.3, ("rows_lo", 2), ("q", 0))
            a("v", 0, TE, 1.3, ("rows_lo", 2), ("k", 0))
            a("q_full", 0, VE, 0.7, ("q", 0))
            a("q_hi", 0, SC, 0.6, ("q_full", 0))
            a("q_lo", 0, PO, 1.2, ("q_hi", 0))
            a("k_full", 0, SC, 0.7, ("k", 0))
            a("k_hi", 0, SC, 0.6, ("k_full", 0))
            a("k_lo", 0, PO, 1.2, ("k_hi", 0))
            a("v_full", 0, VE, 0.7, ("v", 0))
            a("v_a", 0, SC, 0.6, ("v_full", 0))
            a("v_r", 0, PO, 1.2, ("v_a", 0))
            a("v_b", 0, SC, 0.6, ("v_r", 0))
            a("v_c", 0, PO, 1.2, ("v_b", 0))
            for h in range(HQ):
                a("scores", h, TE, 1.3, ("q_lo", 0), ("k_lo", 0), ("smin", h - 2))
                a("smin", h, VE, 0.7, ("scores", h), ("s_exp", h - 2), ("v_r", 0) if h == 1 else None)
                a("s_exp", h, SC, 0.7, ("smin", h), ("p_lo", h - 2), ("v_c", 0) if h == 1 else None)
                a("p_hi", h, SC, 0.5, ("s_exp", h), ("p_T", h - 2))
                a("p_lo", h, PO, 1.2, ("p_hi", h))
                a("p_T", h, TE, 0.45, ("p_lo", h), ("p_copy", h - 1) if h else ("v_full", 0))
                a("p_copy", h, VE, 0.6, ("p_T", h), ("values", h - 1))
                a("values", h, TE, 0.35, ("p_copy", h), ("v_c", 0), ("gather", h // 2 - 1) if h % 2 == 0 else ("values", h - 1))
                if h % 2:
                    a("gather", h // 2, VE, 0.55, ("values", h), ("normal", h // 2 - 1))
                    a("normal", h // 2, VE, 0.25, ("gather", h // 2))
            a("x_bo", 0, PO, 1.2, ("rows", 2), ("v_c", 0))
            transposed(a, TR_CTX, ("normal", HQ // 2 - 1))
            a("wo", 0, TE, 1.3, ("rows_lo", TR_CTX))
            a("x3", 0, VE, 0.6, ("wo", 0), ("x_bo", 0))

        def back(a):
            norm_chain(a, 3, 4, ("x3", 0))
            a("x_beta", 0, PO, 1.2, ("rows", 3))
            for g in range(1, HG + 1):
                graph_attention(a, g, ("rows_lo", 4))
            graph_attention(a, GOUT, ("rows_lo", 4))
            transposed(a, TR_OUT, ("elu", GOUT))
            a("out_b2", 0, PO, 1.2, ("rows_T", TR_OUT))
            a("ffn1", 0, TE, 1.3, ("rows_lo", TR_OUT))
            a("f1_full", 0, SC, 0.7, ("ffn1", 0))
            a("f1_hi", 0, SC, 0.6, ("f1_full", 0))
            a("f1_lo", 0, VE, 0.6, ("f1_hi", 0))
            a("ffn2", 0, TE, 1.3, ("f1_lo", 0))
            a("y", 0, VE, 0.6, ("ffn2", 0), ("out_b2", 0))
            a("stats", 4, VE, 0.65, ("y", 0))
            a("aggr", 4, VE, 0.15, ("stats", 4))
            a("var", 4, VE, 0.08, ("aggr", 4))
            a("inv_std", 4, PO, 0.3, ("var", 4))
            a("y_gamma", 0, VE, 0.7, ("aggr", 4))
            a("final", 0, VE, 0.7, ("y_gamma", 0), ("inv_std", 4), ("x_beta", 0))

        def arrange(chains):
            hop = 0.2
            todo = []
            for s, halves_of in chains:
                known, before = {}, None
                for half in halves_of:
                    names = {}

                    def a(name, k, engine, cost, *after):
                        keep = [(names.get(p) or known.get(p)) for p in after if p is not None]
                        todo.append(dict(step=(name, s, k), engine=engine, cost=cost, rest=0.0, at=None,
                                         after=[p for p in keep if p is not None]
                                         + ([before] if before and len(names) < 2 else [])))
                        names[(name, k)] = todo[-1]

                    half(a)
                    known.update(names)
                    if half is back:
                        known, before = {}, names[("final", 0)]
            for st in reversed(todo):
                st["rest"] += st["cost"] + hop
                for p in st["after"]:
                    p["rest"] = max(p["rest"], st["rest"])
            free, order = [0.0] * 4, []
            while todo:
                best = None
                for st in todo:
                    if all(p["at"] is not None for p in st["after"]):
                        start = max([free[st["engine"]]] + [p["at"] + p["cost"] + hop for p in st["after"]])
                        key = (round(start / GRAIN), -st["rest"])
                        if best is None or key < best[0]:
                            best = (key, start, st)
                _, start, st = best
                st["at"] = start
                free[st["engine"]] = start + st["cost"]
                order.append(st["step"])
                todo.remove(st)
            return order

        GRAIN = 0.4
        def nth(s, k, front_n, n):
            if s == 0:
                return k + 1
            return k - front_n + 1 if k >= front_n else k + n - front_n + 1

        TR_CTX, TR_OUT = 3, 5
        LN_TR = (0, 1, 2, 4)

        def row(s, t):
            return nth(s, t, 4, 6)

        def norm(s, n):
            return nth(s, n, 3, 5)

        def gat(s, g):
            return nth(s, g, 1, HG + 2)

        rows_ready, rows_T, rows_hi, rows_lo = (sem2(n) for n in ("rows_ready", "rows_T", "rows_hi", "rows_lo"))
        var_ready, rstd_ready = sem2("var_ready"), sem2("rstd_ready")
        deg_ready, bo_ready, beta_ready = sem2("deg_ready"), sem2("bo_ready"), sem2("beta_ready")
        mj_done, mi_done, mj_hi, mj_lo, amj_done = (sem2(n) for n in ("mj_done", "mi_done", "mj_hi", "mj_lo", "amj_done"))
        wh_done, wh_hi, wh_lo = sem2("wh_done"), sem2("wh_hi"), sem2("wh_lo")
        dbc_done, tmin_done, bias_ready, exp_done = sem2("dbc_done"), sem2("tmin_done"), sem2("bias_ready"), sem2("exp_done")
        sum_ready, prob_ready = sem2("sum_ready"), sem2("prob_ready")
        pT_done, pT_hi, pT_lo, pv_done = sem2("pT_done"), sem2("pT_hi"), sem2("pT_lo"), sem2("pv_done")
        elu_relu, elu_exp, elu_done, hid_hi, hid_lo = (sem2(n) for n in ("elu_relu", "elu_exp", "elu_done", "hid_hi", "hid_lo"))
        qkv_done = sem2("qkv_done")
        q_full, q_hi, q_lo = sem2("q_full"), sem2("q_hi"), sem2("q_lo")
        k_full, k_hi, k_lo = sem2("k_full"), sem2("k_hi"), sem2("k_lo")
        v_full, v_a, v_r = sem2("v_full"), sem2("v_a"), sem2("v_r")
        v_b, v_c = sem2("v_b"), sem2("v_c")
        s_done, min_ready, p_done, p_hi, p_lo = (sem2(n) for n in ("s_done", "min_ready", "p_done", "p_hi", "p_lo"))
        p16_done, pT16_ready, o_done, o_used = (sem2(n) for n in ("p16_done", "pT16_ready", "o_done", "o_used"))
        wo_done = sem2("wo_done")
        f1_done, f1_full, f1_hi, f1_lo, f2_done = (sem2(n) for n in ("f1_done", "f1_full", "f1_hi", "f1_lo", "f2_done"))
        ob_ready, x_final = sem2("ob_ready"), sem2("x_final")
        loaded = sem("loaded")
        vstep = sem("vstep")
        sems += [loaded, vstep]
        nums = sorted(q.num for q in sems)
        assert nums == list(range(nums[0], nums[-1] + 1))

        def out_rows(b):
            return out[b].rearrange("(c p) d -> p c d", p=P)

        def run_steps(block, order, i):

            @block.sync
            def _(sp):
                if i is None:
                    sp.wait_ge(x_final[1], 1)
                    sp.dma_start(out_rows(B - 1), xs[1][:]).then_inc(stored[1], 16)
                    return
                sp.wait_ge(x_final[1], 1)
                last = sp.snap((i * 2 + B - 1) % B)
                sp.dma_start(out_rows(last), xs[1][:]).then_inc(stored[1], 16)
                for s in S2:
                    if s == 1:
                        sp.wait_ge(x_final[0], 1)
                        cur = sp.snap(i * 2)
                        sp.dma_start(out_rows(cur), xs[0][:]).then_inc(stored[0], 16)
                    sp.wait_ge(rows_ready[s], row(s, 0))
                    sp.wait_ge(deg_ready[s], 1)
                    nxt = sp.snap((i * 2 + 2 + s) % B)
                    sp.dma_start(xin[s][:], x[nxt].rearrange("(c p) d -> p c d", p=P)).then_inc(loaded, 16)
                sp.wait_ge(loaded, 32)

            @block.gpsimd
            def _(pool):
                def inv_std(s, n):
                    pool.wait_ge(var_ready[s], norm(s, n))
                    pool.tensor_tensor(rstd[s][:], ve[s][:], pow_half[:], ALU.pow).then_inc(rstd_ready[s], 1)

                def x_deg(s, _):
                    if s == 1:
                        pool.wait_ge(x_final[s], 1)
                    pool.tensor_tensor(e2[s][:], xin[s][:], degb[:], ALU.add).then_inc(deg_ready[s], 1)

                def scale(s, g):
                    pool.wait_ge(sum_ready[s], gat(s, g))
                    for c in range(C):
                        last = pool.tensor_scalar(pr[s][:, c, :], pr[s][:, c, :], rs[g % 2][s][:, c:c + 1],
                                                  has[:, c:c + 1] if g == 0 else 1.0, ALU.mult, ALU.mult)
                    last.then_inc(prob_ready[s], 1)

                def low_of_q(s, _):
                    pool.wait_ge(q_hi[s], 1)
                    pool.tensor_tensor(hid[s][:, 1, 0:C, :], fu[s][:], f(hid[s][:, 0, 0:C, :]), ALU.subtract)\
                        .then_inc(q_lo[s], 1)

                def low_of_k(s, _):
                    pool.wait_ge(k_hi[s], 1)
                    pool.tensor_tensor(hid[s][:, 1, C:2 * C, :], rb[s][:], f(hid[s][:, 0, C:2 * C, :]),
                                       ALU.subtract).then_inc(k_lo[s], 1)

                def value_rest(s, _):
                    pool.wait_ge(v_a[s], 1)
                    pool.tensor_tensor(e2[s][:], e1[s][:], v_part(s, 0), ALU.subtract).then_inc(v_r[s], 1)

                def value_third(s, _):
                    pool.wait_ge(v_b[s], 1)
                    pool.tensor_tensor(v_part(s, 2), as_heads(e2[s]), v_part(s, 1), ALU.subtract)\
                        .then_inc(v_c[s], 1)

                def x_bo(s, _):
                    pool.wait_ge(rows_ready[s], row(s, 2))
                    pool.tensor_tensor(xs[s][:], xs[s][:], bo_nan[:], ALU.add).then_inc(bo_ready[s], 1)

                def low_of_probs(s, h):
                    pool.wait_ge(p_hi[s], h + 1)
                    pool.tensor_tensor(p16[s][h % 2][:, 1], l2_probs(s, h)[:], p16[s][h % 2][:, 0],
                                       ALU.subtract).then_inc(p_lo[s], 1)

                def x_beta(s, _):
                    pool.wait_ge(rows_ready[s], row(s, 4))
                    for c in range(C):
                        last = pool.tensor_tensor(xs[s][:, c, :], xs[s][:, c, :], beta_b[:], ALU.add)
                    last.then_inc(beta_ready[s], 1)

                def low_of_hidden(s, g):
                    pool.wait_ge(hid_hi[s], g)
                    c0 = C * (g - 1)
                    pool.tensor_tensor(hid[s][:, 1, c0:c0 + C, :], fu[s][:], f(hid[s][:, 0, c0:c0 + C, :]),
                                       ALU.subtract).then_inc(hid_lo[s], 1)

                def out_b2(s, _):
                    pool.wait_ge(rows_T[s], row(s, TR_OUT))
                    for c in range(C):
                        last = pool.tensor_tensor(fu[s][:, c, :], fu[s][:, c, :], b2_b[:], ALU.add)
                    last.then_inc(ob_ready[s], 1)

                program = dict(inv_std=inv_std, x_deg=x_deg, scale=scale, q_lo=low_of_q, k_lo=low_of_k,
                               v_r=value_rest, v_c=value_third, x_bo=x_bo, p_lo=low_of_probs, x_beta=x_beta,
                               hid_lo=low_of_hidden, out_b2=out_b2)
                for name, s, k in order:
                    if name in program:
                        program[name](s, k)

            @block.scalar
            def _(act):
                def high_of_rows(s, t):
                    act.wait_ge(rows_T[s], row(s, t))
                    act.activation(hT[s][:, 0], bank(s, BD if t == TR_OUT else BC),
                                   ACT.Relu if t in LN_TR else ACT.Copy).then_inc(rows_hi[s], 1)

                def high_of_mj(s, _):
                    act.wait_ge(mj_done[s], 1)
                    act.activation(whs[s][1][:, 0], bank(s, BA), ACT.Copy).then_inc(mj_hi[s], 1)

                def high_of_weights(s, g):
                    act.wait_ge(wh_done[s], gat(s, g))
                    if g >= 3:
                        act.wait_ge(pv_done[s], gat(s, g - 2))
                    act.activation(whs[s][g % 2][:, 0], wh_banks(s)[:, :, 0:D], ACT.Copy).then_inc(wh_hi[s], 1)

                def exps(s, g):
                    act.wait_ge(bias_ready[s], gat(s, g))
                    if g >= 2:
                        act.wait_ge(sum_ready[s], gat(s, g - 1))
                    for c in range(C):
                        act.activation(e1[s][:, c, :], tb[s][:, c, :], ACT.Exp,
                                       bias=bias1[g % 2][s][:, c:c + 1], scale=-1.0)
                        last = act.activation(e2[s][:, c, :], tb[s][:, c, :], ACT.Exp,
                                              bias=bias2[g % 2][s][:, c:c + 1], scale=-SLOPE[g])
                    last.then_inc(exp_done[s], 1)

                def high_of_attention(s, g):
                    act.wait_ge(pT_done[s], gat(s, g))
                    if g >= 2:
                        act.wait_ge(pv_done[s], gat(s, g - 1))
                    act.activation(pT[s][:, 0], bank(s, BD), ACT.Copy).then_inc(pT_hi[s], 1)

                def relu_of_negated(s, g):
                    act.wait_ge(pv_done[s], gat(s, g))
                    if g >= 2:
                        act.wait_ge(elu_done[s], g - 1)
                    act.activation(rb[s][:], bank(s, BD if g < GOUT else BC), ACT.Relu, scale=-1.0)\
                        .then_inc(elu_relu[s], 1)

                def elu_exponential(s, g):
                    act.wait_ge(elu_relu[s], g)
                    act.activation(rb[s][:], rb[s][:], ACT.Exp, scale=-1.0).then_inc(elu_exp[s], 1)

                def high_of_q(s, _):
                    act.wait_ge(q_full[s], 1)
                    act.activation(hid[s][:, 0, 0:C, :], fu[s][:], ACT.Copy).then_inc(q_hi[s], 1)

                def whole_k(s, _):
                    act.wait_ge(qkv_done[s], 2)
                    for c in range(C):
                        act.activation(rb[s][:, c, :], bank(s, BB)[:, c, :], ACT.Identity,
                                       bias=bk_c[:, c:c + 1]).then_inc(k_full[s], 1)

                def high_of_k(s, _):
                    act.wait_ge(k_full[s], C)
                    act.activation(hid[s][:, 0, C:2 * C, :], rb[s][:], ACT.Copy).then_inc(k_hi[s], 1)

                def value_first(s, _):
                    act.wait_ge(v_full[s], 1)
                    act.activation(v_part(s, 0), as_heads(e1[s]), ACT.Copy).then_inc(v_a[s], 1)

                def value_second(s, _):
                    act.wait_ge(v_r[s], 1)
                    act.activation(v_part(s, 1), as_heads(e2[s]), ACT.Copy).then_inc(v_b[s], 1)

                def softmax_exp(s, h):
                    act.wait_ge(min_ready[s], h + 1)
                    if h == 1:
                        act.wait_ge(v_c[s], 1)
                    if h >= 2:
                        act.wait_ge(p_lo[s], h - 1)
                    for c in range(C):
                        last = act.activation(l2_probs(s, h)[:, c, :], l2_logits(s, h)[:, c, :], ACT.Exp,
                                              bias=hmin[s][h % 2][:, c:c + 1], scale=-1.0)
                    last.then_inc(p_done[s], 1)

                def high_of_probs(s, h):
                    act.wait_ge(p_done[s], h + 1)
                    if h >= 2:
                        act.wait_ge(p16_done[s], h - 1)
                    act.activation(p16[s][h % 2][:, 0], l2_probs(s, h)[:], ACT.Copy).then_inc(p_hi[s], 1)

                def high_of_hidden(s, g):
                    act.wait_ge(elu_done[s], g)
                    act.activation(hid[s][:, 0, C * (g - 1):C * g, :], fu[s][:], ACT.Copy).then_inc(hid_hi[s], 1)

                def whole_ffn(s, _):
                    act.wait_ge(f1_done[s], 1)
                    for c in range(C):
                        act.activation(rb[s][:, c, :], bank(s, BA)[:, c, :], ACT.Relu,
                                       bias=b1_c[:, c:c + 1]).then_inc(f1_full[s], 1)

                def high_of_ffn(s, _):
                    act.wait_ge(f1_full[s], C)
                    act.activation(hid[s][:, 0, 0:C, :], rb[s][:], ACT.Copy).then_inc(f1_hi[s], 1)

                program = dict(rows_hi=high_of_rows, mj_hi=high_of_mj, wh_hi=high_of_weights, exps=exps,
                               probs_hi=high_of_attention, elu_relu=relu_of_negated, elu_exp=elu_exponential,
                               q_hi=high_of_q, k_full=whole_k, k_hi=high_of_k, v_a=value_first,
                               v_b=value_second, s_exp=softmax_exp, p_hi=high_of_probs, hid_hi=high_of_hidden,
                               f1_full=whole_ffn, f1_hi=high_of_ffn)
                for name, s, k in order:
                    if name in program:
                        program[name](s, k)

            @block.tensor
            def _(pe):
                def product(dst, lhs, rhs, terms):
                    n = 0
                    for t in range(terms):
                        for a, b in PARTS:
                            last = pe.matmul(dst, lhs(a, t), rhs(b, t), start=(n == 0), stop=(n == 3 * terms - 1))
                            n += 1
                    return last

                def blk(k):
                    return slice(k * P, (k + 1) * P)

                def rows_from(s, k, w):
                    for c in range(C):
                        last = product(bank(s, k)[:, c, :], lambda a, t: hT[s][:, a, t, blk(c)],
                                       lambda b, t: w[:, b, t, :], C)
                    return last

                def columns_from(s, k, w):
                    for c in range(C):
                        last = product(bank(s, k)[:, c, :], lambda a, t: w[:, a, t, blk(c)],
                                       lambda b, t: hT[s][:, b, t, :], C)
                    return last

                def transpose_rows(s, t):
                    k = BD if t == TR_OUT else BC
                    src = pr if t in LN_TR else fu
                    pe.wait_ge(rows_ready[s], row(s, t))
                    for kc in range(C):
                        for c in range(C):
                            last = pe.transpose(bank(s, k)[:, kc, blk(c)], src[s][:, c, blk(kc)], ident[:])
                    last.then_inc(rows_T[s], 1)

                def layer0_neighbours(s, _):
                    pe.wait_ge(rows_lo[s], row(s, 0))
                    rows_from(s, BA, w0[:, :, C:2 * C, :]).then_inc(mj_done[s], 1)

                def layer0_own(s, _):
                    pe.wait_ge(rows_lo[s], row(s, 0))
                    rows_from(s, BB, w0[:, :, 0:C, :]).then_inc(mi_done[s], 1)

                def layer0_sum(s, _):
                    pe.wait_ge(mj_lo[s], 1)
                    for c in range(C):
                        last = product(bank(s, BD)[:, c, :], lambda a, t: at[:, a, t, blk(c)],
                                       lambda b, t: whs[s][1][:, b, t, :], C)
                    last.then_inc(amj_done[s], 1)

                def attention_weights(s, g):
                    if g < 2:
                        pe.wait_ge(rows_lo[s], row(s, 4 if g else 1))
                    else:
                        pe.wait_ge(wh_lo[s], gat(s, g - 1))
                    if g == GOUT:
                        pe.wait_ge(hid_lo[s], HG)
                    for c in range(C):
                        if g == GOUT:
                            last = product(wh_banks(s)[:, c, 0:WC], lambda a, t: hid[s][:, a, t, blk(c)],
                                           lambda b, t: wout[:, b, t, :], HG * C)
                        else:
                            w = w1g[:, :, :, :] if g == 0 else wh[:, :, C * (g - 1):C * g, :]
                            last = product(wh_banks(s)[:, c, 0:WC], lambda a, t: hT[s][:, a, t, blk(c)],
                                           lambda b, t: w[:, b, t, :], C)
                    last.then_inc(wh_done[s], 1)

                def spread_targets(s, g):
                    pe.wait_ge(wh_lo[s], gat(s, g))
                    if g >= 2:
                        pe.wait_ge(tmin_done[s], gat(s, g - 1))
                    for c in range(C):
                        last = pe.matmul(bank(s, BC)[:, 0, blk(c)], cols[g % 2][s][:, c, 1:2].broadcast_to([P, P]),
                                         ident[:], start=True, stop=True)
                    last.then_inc(dbc_done[s], 1)

                def transpose_attention(s, g):
                    pe.wait_ge(prob_ready[s], gat(s, g))
                    if g >= 2:
                        pe.wait_ge(elu_done[s], g - 1)
                    for jc in range(C):
                        for c in range(C):
                            last = pe.transpose(bank(s, BD)[:, jc, blk(c)], pr[s][:, c, blk(jc)], ident[:])
                    last.then_inc(pT_done[s], 1)

                def attend(s, g):
                    pe.wait_ge(pT_lo[s], gat(s, g))
                    w = whs[s][g % 2]
                    for c in range(C):
                        if 1 <= g <= HG:
                            last = product(bank(s, BD)[:, c, :], lambda a, t: w[:, a, t, blk(c)],
                                           lambda b, t: pT[s][:, b, t, :], C)
                        else:
                            last = product(bank(s, BC)[:, c, :], lambda a, t: pT[s][:, a, t, blk(c)],
                                           lambda b, t: w[:, b, t, :], C)
                    last.then_inc(pv_done[s], 1)

                def query(s, _):
                    pe.wait_ge(rows_lo[s], row(s, 2))
                    columns_from(s, BA, wq).then_inc(qkv_done[s], 1)

                def key(s, _):
                    columns_from(s, BB, wk).then_inc(qkv_done[s], 1)

                def value(s, _):
                    rows_from(s, BC, wv).then_inc(qkv_done[s], 1)

                def scores(s, h):
                    if h == 0:
                        pe.wait_ge(q_lo[s], 1)
                        pe.wait_ge(k_lo[s], 1)
                    if h >= 2:
                        pe.wait_ge(min_ready[s], h - 1)
                    r, oc = slice(DH * (h % 4), DH * (h % 4) + DH), h // 4
                    for c in range(C):
                        for n, (a, b) in enumerate(PARTS):
                            last = pe.matmul(bank(s, h % 2)[:, c, :], hid[s][r, a, oc, blk(c)],
                                             hid[s][r, b, C + oc, :], start=(n == 0), stop=(n == 2))
                    last.then_inc(s_done[s], 1)

                def transpose_probs(s, h):
                    pe.wait_ge(p_lo[s], h + 1)
                    if h == 0:
                        pe.wait_ge(v_full[s], 1)
                    else:
                        pe.wait_ge(pT16_ready[s], h)
                    for part in range(2):
                        for kc in range(C):
                            for c in range(C):
                                last = pe.transpose(bank16(s, BC)[:, part, kc, blk(c)],
                                                    p16[s][h % 2][:, part, c, blk(kc)], ident16[:])
                    last.then_inc(p16_done[s], 1)

                def values(s, h):
                    pe.wait_ge(pT16_ready[s], h + 1)
                    if h == 0:
                        pe.wait_ge(v_c[s], 1)
                    if h % 2 == 0 and h:
                        pe.wait_ge(o_used[s], h // 2)
                    for c in range(C):
                        at0 = BD * BANK + ((h % 2) * C + c) * VC
                        for n, (part, kc) in enumerate(((0, 0), (0, 1), (1, 0), (1, 1))):
                            last = pe.matmul(ps[s][:, at0:at0 + VC], pT16[s][:, part, kc, blk(c)],
                                             v3[s][:, kc, h, :], start=(n == 0), stop=(n == 2 * C - 1))
                    last.then_inc(o_done[s], 1)

                def context_out(s, _):
                    pe.wait_ge(rows_lo[s], row(s, TR_CTX))
                    rows_from(s, BA, wo).then_inc(wo_done[s], 1)

                def ffn_in(s, _):
                    pe.wait_ge(rows_lo[s], row(s, TR_OUT))
                    columns_from(s, BA, wf1).then_inc(f1_done[s], 1)

                def ffn_out(s, _):
                    pe.wait_ge(f1_lo[s], 1)
                    for c in range(C):
                        last = product(bank(s, BB)[:, c, :], lambda a, t: hid[s][:, a, t, blk(c)],
                                       lambda b, t: wf2[:, b, t, :], C)
                    last.then_inc(f2_done[s], 1)

                program = dict(rows_T=transpose_rows, mj=layer0_neighbours, mi=layer0_own, amj=layer0_sum,
                               wh=attention_weights, spread=spread_targets, probs_T=transpose_attention,
                               attend=attend, q=query, k=key, v=value, scores=scores, p_T=transpose_probs,
                               values=values, wo=context_out, ffn1=ffn_in, ffn2=ffn_out)
                for name, s, k in order:
                    if name in program:
                        program[name](s, k)

            @block.vector
            def _(dve):
                marks = {}
                count = [0]

                def mark(ins, key):
                    count[0] += 1
                    ins.then_inc(vstep, 1)
                    marks[key] = count[0]

                def after(key):
                    if key in marks:
                        dve.wait_ge(vstep, marks[key])

                def norm_src(s, n):
                    return xin[s] if n == 0 else e1[s] if n == 4 else xs[s]

                def stats_of(s, n):
                    after(("y" if n == 4 else "x", s))
                    for c in range(C):
                        last = dve.bn_stats(stats[s][:, c, :], norm_src(s, n)[:, c, :])
                    mark(last, ("stats", s))

                def aggregate(s, n):
                    after(("stats", s))
                    for c in range(C):
                        last = dve.bn_aggr(mv[s][:, c, :], stats[s][:, c, :])
                    mark(last, ("aggr", s))

                def variance(s, n):
                    after(("aggr", s))
                    dve.tensor_scalar(ve[s][:], mv[s][:, :, 1], EPS, None, ALU.add).then_inc(var_ready[s], 1)

                def norm_rows(s, n):
                    dve.wait_ge(rstd_ready[s], norm(s, n))
                    for c in range(C):
                        last = dve.tensor_scalar(pr[s][:, c, :], norm_src(s, n)[:, c, :], mv[s][:, c, 0:1],
                                                 rstd[s][:, c:c + 1], ALU.subtract, ALU.mult)
                    last.then_inc(rows_ready[s], 1)

                def low_of_rows(s, t):
                    dve.wait_ge(rows_hi[s], row(s, t))
                    src = bank(s, BD if t == TR_OUT else BC)
                    dst, hi = hT[s][:, 1], f(hT[s][:, 0])
                    if t in LN_TR:
                        ins = dve.scalar_tensor_tensor(out=dst, in0=src, scalar=0.0, in1=hi,
                                                       op0=ALU.max, op1=ALU.subtract)
                    else:
                        ins = dve.tensor_tensor(dst, src, hi, ALU.subtract)
                    ins.then_inc(rows_lo[s], 1)

                def low_of_mj(s, _):
                    dve.wait_ge(mj_hi[s], 1)
                    dve.tensor_tensor(whs[s][1][:, 1], bank(s, BA), f(whs[s][1][:, 0]), ALU.subtract)\
                        .then_inc(mj_lo[s], 1)

                def x_plus_own(s, _):
                    dve.wait_ge(stored[s], dve.snap(i * 16 + 16))
                    dve.wait_ge(mi_done[s], 1)
                    dve.wait_ge(deg_ready[s], 1)
                    for c in range(C):
                        last = dve.scalar_tensor_tensor(out=xs[s][:, c, :], in0=bank(s, BB)[:, c, :],
                                                        scalar=deg[:, c:c + 1], in1=e2[s][:, c, :],
                                                        op0=ALU.mult, op1=ALU.add)
                    mark(last, ("x", s))

                def x_plus(done, value_of, k):
                    def add(s, _):
                        dve.wait_ge(done[s], value_of(s))
                        if k == BA:
                            dve.wait_ge(bo_ready[s], 1)
                        after(("x", s))
                        mark(dve.tensor_tensor(xs[s][:], xs[s][:], bank(s, k), ALU.add), ("x", s))
                    return add

                def low_of_weights(s, g):
                    dve.wait_ge(wh_hi[s], gat(s, g))
                    mark(dve.tensor_copy(cols[g % 2][s][:], wh_banks(s)[:, :, D:WC]), ("cols", s, g))
                    dve.tensor_tensor(whs[s][g % 2][:, 1], wh_banks(s)[:, :, 0:D],
                                      f(whs[s][g % 2][:, 0]), ALU.subtract).then_inc(wh_lo[s], 1)

                def masked_minimum(s, g):
                    m = maskp if g == 0 else mask3p
                    dve.wait_ge(dbc_done[s], gat(s, g))
                    if g >= 2:
                        dve.wait_ge(exp_done[s], gat(s, g - 1))
                    for c in range(C):
                        last = dve.tensor_tensor_reduce(
                            out=tb[s][:, c, :], in0=bank(s, BC)[:, 0, :], in1=m[:, c, :], scale=1.0,
                            scalar=3.0e38, op0=ALU.add, op1=ALU.min, accum_out=dmin[s][:, c:c + 1])
                    last.then_inc(tmin_done[s], 1)

                def top_logit(s, g):
                    dve.wait_ge(tmin_done[s], gat(s, g))
                    mark(dve.tensor_tensor(zz[s][:], cols[g % 2][s][:, :, 0], dmin[s][:], ALU.subtract), ("zz", s))

                def leaky_top(s, g):
                    after(("zz", s))
                    mark(dve.scalar_tensor_tensor(out=mm[s][:], in0=zz[s][:], scalar=SLOPE[g], in1=zz[s][:],
                                                  op0=ALU.mult, op1=ALU.max), ("mm", s))

                def exp_biases(s, g):
                    after(("mm", s))
                    src = cols[g % 2][s][:, :, 0]
                    mark(dve.tensor_tensor(bias1[g % 2][s][:], src, mm[s][:], ALU.subtract), ("bias", s))
                    dve.scalar_tensor_tensor(out=bias2[g % 2][s][:], in0=src, scalar=SLOPE[g], in1=mm[s][:],
                                             op0=ALU.mult, op1=ALU.subtract).then_inc(bias_ready[s], 1)

                def larger_branch(s, g):
                    dve.wait_ge(exp_done[s], gat(s, g))
                    if g >= 2:
                        dve.wait_ge(pT_done[s], gat(s, g - 1))
                    for c in range(C):
                        last = dve.scalar_tensor_tensor(out=pr[s][:, c, :], in0=e1[s][:, c, :], scalar=1.0,
                                                        in1=e2[s][:, c, :], op0=ALU.mult, op1=ALU.max,
                                                        accum_out=psums[s][:, c:c + 1])
                    mark(last, ("psums", s))

                def inverse_sums(s, g):
                    after(("psums", s))
                    dve.reciprocal(rs[g % 2][s][:], psums[s][:]).then_inc(sum_ready[s], 1)

                def low_of_attention(s, g):
                    dve.wait_ge(pT_hi[s], gat(s, g))
                    dve.tensor_tensor(pT[s][:, 1], bank(s, BD), f(pT[s][:, 0]), ALU.subtract)\
                        .then_inc(pT_lo[s], 1)

                def elu(s, g):
                    dve.wait_ge(elu_exp[s], g)
                    if g >= 2:
                        dve.wait_ge(hid_lo[s], g - 1)
                    dve.scalar_tensor_tensor(out=fu[s][:], in0=rb[s][:], scalar=-1.0,
                                             in1=bank(s, BD if g < GOUT else BC), op0=ALU.add, op1=ALU.max)\
                        .then_inc(elu_done[s] if g < GOUT else rows_ready[s], 1)

                def whole_q(s, _):
                    dve.wait_ge(qkv_done[s], 1)
                    for c in range(C):
                        last = dve.tensor_scalar(fu[s][:, c, :], bank(s, BA)[:, c, :], bq_c[:, c:c + 1], -SCALE,
                                                 ALU.add, ALU.mult)
                    last.then_inc(q_full[s], 1)

                def whole_v(s, _):
                    dve.wait_ge(qkv_done[s], 3)
                    for c in range(C):
                        last = dve.tensor_tensor(e1[s][:, c, :], bank(s, BC)[:, c, :], bv_b[:], ALU.add)
                    last.then_inc(v_full[s], 1)

                def score_minimum(s, h):
                    dve.wait_ge(s_done[s], h + 1)
                    if h == 1:
                        dve.wait_ge(v_r[s], 1)
                    if h >= 2:
                        dve.wait_ge(p_done[s], h - 1)
                    for c in range(C):
                        last = dve.tensor_tensor_reduce(
                            out=l2_logits(s, h)[:, c, :], in0=bank(s, h % 2)[:, c, :], in1=maskp[:, c, :],
                            scale=1.0, scalar=3.0e38, op0=ALU.add, op1=ALU.min,
                            accum_out=hmin[s][h % 2][:, c:c + 1])
                    last.then_inc(min_ready[s], 1)

                def copy_probs(s, h):
                    dve.wait_ge(p16_done[s], h + 1)
                    if h:
                        dve.wait_ge(o_done[s], h)
                    dve.tensor_copy(pT16[s][:], bank16(s, BC)).then_inc(pT16_ready[s], 1)

                def two_heads(s, p):
                    return fu[s][:, :, 2 * p * DH:(2 * p + 2) * DH].rearrange("p c (h d) -> p h c d", h=2)

                def gather_values(s, p):
                    dve.wait_ge(o_done[s], 2 * p + 2)
                    after(("ctx", s))
                    o = ps[s][:, BD * BANK:BD * BANK + 2 * C * VC].rearrange("p (g v) -> p g v", v=VC)
                    mark(dve.reciprocal(rden[s][:], o[:, :, 3 * DH]), ("rden", s))
                    for hh in range(2):
                        last = dve.tensor_reduce(
                            out=two_heads(s, p)[:, hh], axis=AX.X, op=ALU.add,
                            in_=o[:, hh * C:hh * C + C, 0:3 * DH].rearrange("p c (t d) -> p c d t", t=3))
                    last.then_inc(o_used[s], 1)

                def normalise(s, p):
                    dve.wait_ge(o_used[s], p + 1)
                    for hh in range(2):
                        r = rden[s][:, hh * C:hh * C + C].rearrange("p (c o) -> p c o", o=1)
                        last = dve.tensor_tensor(two_heads(s, p)[:, hh], two_heads(s, p)[:, hh],
                                                 r.broadcast_to([P, C, DH]), ALU.mult)
                    if p == HQ // 2 - 1:
                        last.then_inc(rows_ready[s], 1)
                    else:
                        mark(last, ("ctx", s))

                def low_of_ffn(s, _):
                    dve.wait_ge(f1_hi[s], 1)
                    dve.tensor_tensor(hid[s][:, 1, 0:C, :], rb[s][:], f(hid[s][:, 0, 0:C, :]), ALU.subtract)\
                        .then_inc(f1_lo[s], 1)

                def ffn_sum(s, _):
                    dve.wait_ge(f2_done[s], 1)
                    dve.wait_ge(ob_ready[s], 1)
                    mark(dve.tensor_tensor(e1[s][:], fu[s][:], bank(s, BB), ALU.add), ("y", s))

                def times_gamma(s, _):
                    after(("aggr", s))
                    for c in range(C):
                        last = dve.scalar_tensor_tensor(out=e2[s][:, c, :], in0=e1[s][:, c, :],
                                                        scalar=mv[s][:, c, 0:1], in1=gamma_b[:],
                                                        op0=ALU.subtract, op1=ALU.mult)
                    mark(last, ("yg", s))

                def result(s, _):
                    after(("yg", s))
                    dve.wait_ge(rstd_ready[s], norm(s, 4))
                    dve.wait_ge(beta_ready[s], 1)
                    for c in range(C):
                        last = dve.scalar_tensor_tensor(out=xs[s][:, c, :], in0=e2[s][:, c, :],
                                                        scalar=rstd[s][:, c:c + 1], in1=xs[s][:, c, :],
                                                        op0=ALU.mult, op1=ALU.add)
                    last.then_inc(x_final[s], 1)

                program = dict(stats=stats_of, aggr=aggregate, var=variance, rows=norm_rows, rows_lo=low_of_rows,
                               mj_lo=low_of_mj, x_mi=x_plus_own, x1=x_plus(amj_done, lambda s: 1, BD),
                               wh_lo=low_of_weights, tmin=masked_minimum, top=top_logit, leaky_top=leaky_top,
                               biases=exp_biases, larger=larger_branch, inv_sum=inverse_sums,
                               probs_lo=low_of_attention, elu=elu,
                               x2=x_plus(pv_done, lambda s: gat(s, 0), BC), q_full=whole_q, v_full=whole_v,
                               smin=score_minimum, p_copy=copy_probs, gather=gather_values, normal=normalise,
                               x3=x_plus(wo_done, lambda s: 1, BA), f1_lo=low_of_ffn, y=ffn_sum,
                               y_gamma=times_gamma, final=result)
                for name, s, k in order:
                    if name in program:
                        program[name](s, k)

        order = arrange(((0, (front, back)), (1, (back, front))))
        with nc.Fori(0, LOOPS) as i:
            with nc.Block(no_gpsimd_drain=True) as block:
                run_steps(block, order, i)
            nc.all_engine_barrier(sems_to_clear=range(nums[0], nums[-1] + 1))

        with nc.Block() as block:
            run_steps(block, arrange(((1, (back,)),)), None)
        with nc.Block() as block:
            @block.sync
            def _(sp):
                sp.wait_ge(stored[0], 16 * LOOPS + 16)
                sp.wait_ge(stored[1], 16 * LOOPS + 16)


def kernel(**inputs):
    import numpy as np
    import concourse.bacc as bacc
    from concourse import mybir as _mybir
    from concourse.bass_utils import run_bass_kernel_spmd

    def t(a):
        return np.ascontiguousarray(np.asarray(a).T)

    g = {k: np.ascontiguousarray(np.asarray(v)) for k, v in inputs.items()}
    arrays = {
        "x_in": g["x"], "adj": g["adj"], "adj_t": t(g["adj"]),
        "L0_W_t": t(g["L0_gnn_W"]), "L0_b": g["L0_gnn_b"],
        "L1_W": g["L1_gnn_W"], "L1_a_src": g["L1_gnn_a_src"], "L1_a_dst": g["L1_gnn_a_dst"],
        "Wq_t": t(g["L2_gnn_Wq"]), "bq": g["L2_gnn_bq"], "Wk_t": t(g["L2_gnn_Wk"]), "bk": g["L2_gnn_bk"],
        "Wv_t": t(g["L2_gnn_Wv"]), "bv": g["L2_gnn_bv"], "Wo_t": t(g["L2_gnn_Wo"]), "bo": g["L2_gnn_bo"],
        "W_heads": g["L3_gnn_W_heads"], "a_heads": g["L3_gnn_a_heads"], "W_out": g["L3_gnn_W_out"],
        "a_out": g["L3_gnn_a_out"], "w1": g["L3_gnn_w1"], "b1": g["L3_gnn_b1"], "w2": g["L3_gnn_w2"],
        "b2": g["L3_gnn_b2"], "gamma": g["L3_gnn_ln_gamma"], "beta": g["L3_gnn_ln_beta"],
    }
    nc = bacc.Bacc("TRN2", target_bir_lowering=False, num_devices=1)
    args = [nc.dram_tensor(k, a.shape, _mybir.dt.from_np(a.dtype), kind="ExternalInput").ap()
            for k, a in arrays.items()]
    out = nc.dram_tensor("out", g["x"].shape, _mybir.dt.float32, kind="ExternalOutput").ap()
    adj_preln_kernel(nc, *args, out)
    r = run_bass_kernel_spmd(nc, [arrays], core_ids=[0])
    return r.results[0]["out"]
```

```python
import concourse.bass as bass
from concourse import mybir
from contextlib import ExitStack


def adj_preln_kernel(nc, x, adj, adj_t, L0_W_t, L0_b, L1_W, L1_a_src, L1_a_dst,
                     Wq_t, bq, Wk_t, bk, Wv_t, bv, Wo_t, bo,
                     W_heads, a_heads, W_out, a_out, w1, b1, w2, b2, gamma, beta, out):
    F32, F32R = mybir.dt.float32, mybir.dt.float32r
    F16, BF16, I32 = mybir.dt.float16, mybir.dt.bfloat16, mybir.dt.int32
    ALU, ACT, AX = mybir.AluOpType, mybir.ActivationFunctionType, mybir.AxisListType

    B, N, D = x.shape
    P = 128
    C = N // P
    assert N == D == 2 * P and B % 2 == 0
    HQ = 8
    DH = D // HQ
    HG = W_heads.shape[0]
    SCALE = float(DH) ** -0.5
    BIG = 1.0e30
    EPS = 1e-5
    SLOPE = [0.2] + [0.01] * (HG + 1)
    GOUT = HG + 1
    WC = D + 2
    VC = 3 * DH + 1
    S2 = (0, 1)
    BANK = 512
    PARTS = ((0, 0), (0, 1), (1, 0))
    ROUNDS = 2
    LOOPS = B // (2 * ROUNDS)
    assert LOOPS * 2 * ROUNDS == B

    ctx = ExitStack()
    with ctx:
        def sb(name, shape, dt=F32):
            return ctx.enter_context(nc.sbuf_tensor(name, shape, dt))

        def sem(name):
            return ctx.enter_context(nc.semaphore(name))

        sems = []

        def sem2(name):
            pair = [sem(f"{name}{s}") for s in S2]
            sems.extend(pair)
            return pair

        w0 = sb("w0", [P, 2, 2 * C, D], F32R)
        w1g = sb("w1g", [P, 2, C, WC], F32R)
        wq = sb("wq", [P, 2, C, D], F32R)
        wk = sb("wk", [P, 2, C, D], F32R)
        wv = sb("wv", [P, 2, C, D], F32R)
        wo = sb("wo", [P, 2, C, D], F32R)
        wh = sb("wh", [P, 2, HG * C, WC], F32R)
        wout = sb("wout", [P, 2, HG * C, WC], F32R)
        wf1 = sb("wf1", [P, 2, C, D], F32R)
        wf2 = sb("wf2", [P, 2, C, D], F32R)
        at = sb("at", [P, 2, C, N], F32R)
        maskp = sb("maskp", [P, C, N])
        mask3p = sb("mask3p", [P, C, N])
        deg = sb("deg", [P, C])
        has = sb("has", [P, C])
        degb = sb("degb", [P, C, D])
        bo_nan = sb("bo_nan", [P, C, D])
        bv_b = sb("bv_b", [P, D])
        b2_b = sb("b2_b", [P, D])
        gamma_b = sb("gamma_b", [P, D])
        beta_b = sb("beta_b", [P, D])
        bq_c = sb("bq_c", [P, C])
        bk_c = sb("bk_c", [P, C])
        b1_c = sb("b1_c", [P, C])
        ident = sb("ident", [P, P])
        ident16 = sb("ident16", [P, P], F16)

        pow_half = sb("pow_half", [P, C])

        def per(name, shape, dt=F32):
            return [sb(f"{name}_{s}", shape, dt) for s in S2]

        xin = per("xin", [P, C, D])
        xs = per("xs", [P, C, D])
        tb = per("tb", [P, C, N])
        e1 = per("e1", [P, C, N])
        e2 = per("e2", [P, C, N])
        pr = per("pr", [P, C, N])
        rb = per("rb", [P, C, N])
        fu = per("fu", [P, C, N])
        hT = per("hT", [P, 2, C, N], F32R)
        whs = [[sb(f"whs{k}_{s}", [P, 2, C, D], F32R) for k in range(HG)] for s in S2]
        pT = per("pT", [P, 2, C, N], F32R)
        hid = per("hid", [P, 2, 2 * C, N], F32R)
        v3 = per("v3", [P, C, HQ, VC], BF16)
        p16 = [[sb(f"p16{k}_{s}", [P, 2, C, N], F16) for k in range(2)] for s in S2]
        pT16 = per("pT16", [P, 2, C, N], F16)
        cols = [per(f"cols{k}", [P, C, 2]) for k in range(HG + 2)]
        dmin = per("dmin", [P, C])
        zz = per("zz", [P, C])
        mm = per("mm", [P, C])
        bias1 = [per(f"bias1{k}", [P, C]) for k in range(2)]
        bias2 = [per(f"bias2{k}", [P, C]) for k in range(2)]
        psums = per("psums", [P, C])
        rs = [per(f"rs{k}", [P, C]) for k in range(2)]
        hmin = [[sb(f"hmin{k}_{s}", [P, C]) for k in range(2)] for s in S2]
        rden = per("rden", [P, 2 * C])
        stats = per("stats", [P, C, 6])
        mv = per("mv", [P, C, 2])
        ve = per("ve", [P, C])
        rstd = per("rstd", [P, C])

        ps = [ctx.enter_context(nc.psum_tensor(f"ps{s}", [P, 4 * BANK], F32)) for s in S2]
        BA, BB, BC, BD = range(4)

        def bank(s, k, n=N):
            return ps[s][:, k * BANK:k * BANK + 2 * n].rearrange("p (c n) -> p c n", c=2)

        def wh_banks(s):
            return ps[s][:, 0:2 * BANK].rearrange("p (c n) -> p c n", c=2)

        def bank16(s, k):
            return ps[s][:, k * BANK:(k + 1) * BANK].bitcast(F16).rearrange("p (t c n) -> p t c n", t=2, c=C)

        def f(t):
            return t.bitcast(F32)

        def wh_parts(s, g):
            return whs[s][(g - 1) % HG if g else 0]

        def hid_part(s, a, g):
            k = C * ((g - 1) % 2)
            return hid[s][:, a, k:k + C, :]

        def layer1_or_head(g):
            return w1g[:] if g == 0 else wh[:, :, C * (g - 1):C * g, :]

        def as_heads(t):
            return t[:].rearrange("p c (h d) -> p c h d", h=HQ)

        def v_part(s, k):
            return v3[s][:, :, :, k * DH:(k + 1) * DH]

        def l2_logits(s, h):
            return (tb, e1)[h % 2][s]

        def l2_probs(s, h):
            return (pr, e2)[h % 2][s]

        stored = [sem("stored0"), sem("stored1")]

        lent = [t[s][:] for t in (tb, e1, e2, pr, rb, fu) for s in S2] + [xs[0][:]]
        adj_i, adjt_i, adj_f, adjt_f, linked = lent[-5:]
        NST = len(lent)
        products = sb("products", [P, 2, C, D])

        def halves(w, k):
            return w[k * D:(k + 1) * D, :].rearrange("(c p) n -> p c n", p=P)

        plain = [(halves(L0_W_t, 0), w0[:, :, 0:C, :], None), (halves(L0_W_t, 1), w0[:, :, C:2 * C, :], None),
                 (halves(Wq_t, 0), wq[:, :, :, :], None), (halves(Wk_t, 0), wk[:, :, :, :], None),
                 (halves(Wv_t, 0), wv[:, :, :, :], None), (halves(Wo_t, 0), wo[:, :, :, :], None),
                 (halves(w1, 0), wf1[:, :, :, :], None), (halves(w2, 0), wf2[:, :, :, :], None)]
        scored = [(halves(L1_W, 0), w1g[:, :, :, :], 0)]
        scored += [(halves(W_heads[h], 0), wh[:, :, C * h:C * h + C, :], 1 + h) for h in range(HG)]
        scored += [(halves(W_out, h), wout[:, :, C * h:C * h + C, :], GOUT) for h in range(HG)]
        units = [u for k in range(max(len(plain), len(scored))) for u in scored[k:k + 1] + plain[k:k + 1]]
        NU = len(units)
        avecs = [(L1_a_src, L1_a_dst)] + [(a_heads[h, 0:D], a_heads[h, D:2 * D]) for h in range(HG)] \
            + [(a_out[0:D], a_out[D:2 * D])]
        avec = [t.bitcast(F32).rearrange("p t c n -> p (t c n)").rearrange("p (k n) -> p k n", k=2)
                for s in S2 for t in (p16[s][0][:], p16[s][1][:], pT16[s][:])]
        assert len(avec) == len(avecs) and NU <= 2 * NST
        stage = [lent[n % NST] for n in range(NU)]

        def bcast(v):
            return v.rearrange("(o n) -> o n", o=1).broadcast_to([P, v.shape[0]])

        def column(v):
            return v.rearrange("(c p) -> p c", p=P)

        staged = [sem(f"staged{k}") for k in range((NU + 1) // 2)]
        vectors_in = sem("vectors_in")
        small = sem("small")
        adj_in = sem("adj_in")
        split_hi = sem("split_hi")
        split_lo = {False: sem("split_lo_scored"), True: sem("split_lo_plain")}
        adjacency_made = sem("adjacency_made")
        made = sem("made")
        pooled = sem("pooled")
        first_x = sem("first_x")
        wcol = sb("wcol", [P, NU, C, 2])

        def all_staged(n):
            return 32 if n | 1 < NU else 16

        with nc.Block() as block:
            @block.sync
            def _(sp):
                def load(n):
                    if NST - 5 <= n < NST:
                        sp.wait_ge(adjacency_made, 1)
                    if n >= NST:
                        is_plain = units[n - NST][2] is None
                        sp.wait_ge(split_lo[is_plain],
                                   sum((g is None) == is_plain for _, _, g in units[:n - NST + 1]))
                    sp.dma_start(stage[n], units[n][0]).then_inc(staged[n // 2], 16)

                sp.sem_inc(stored[0], 16)
                sp.dma_start(adj_i.bitcast(I32), adj.rearrange("(c p) n -> p c n", p=P)).then_inc(adj_in, 16)
                sp.dma_start(adjt_i.bitcast(I32), adj_t.rearrange("(c p) n -> p c n", p=P)).then_inc(adj_in, 16)
                for n in range(4):
                    load(n)
                for k, (a, b) in enumerate(avecs):
                    sp.dma_start(avec[k][:, 0, :], bcast(a)).then_inc(vectors_in, 16)
                    sp.dma_start(avec[k][:, 1, :], bcast(b)).then_inc(vectors_in, 16)
                sp.dma_start(degb[:, 0, :], bcast(L0_b)).then_inc(vectors_in, 16)
                sp.dma_start(bo_nan[:, 0, :], bcast(bo)).then_inc(vectors_in, 16)
                for n in range(4, NST - 5):
                    load(n)
                for dst, v in ((bv_b, bv), (b2_b, b2), (gamma_b, gamma), (beta_b, beta)):
                    sp.dma_start(dst[:], bcast(v)).then_inc(small, 16)
                for dst, v in ((bq_c, bq), (bk_c, bk), (b1_c, b1)):
                    with nc.allow_non_contiguous_dma(reason="bias columns, once"):
                        sp.dma_start(dst[:], column(v)).then_inc(small, 16)
                for s in S2:
                    sp.dma_start(xin[s][:], x[s].rearrange("(c p) d -> p c d", p=P)).then_inc(first_x, 16)
                sp.dma_start(xs[1][:], x[1].rearrange("(c p) d -> p c d", p=P)).then_inc(first_x, 16)
                for n in range(NST - 5, NU):
                    load(n)
                sp.wait_ge(small, 16 * 7)
                sp.wait_ge(first_x, 16 * 3)

            @block.gpsimd
            def _(pool):
                pool.memset(ident[:], 0.0).then_inc(pooled, 1)
                pool.memset(pow_half[:], -0.5).then_inc(pooled, 1)
                for s in S2:
                    pool.memset(v3[s][:], 1.0).then_inc(pooled, 1)
                pool.wait_ge(pooled, 4)
                pool.affine_select(out=ident[:], in_=ident[:], compare_op=ALU.not_equal, fill=1.0, base=0,
                                   pattern=[[-1, P]], channel_multiplier=1).then_inc(pooled, 1)
                pool.wait_ge(pooled, 5)
                pool.tensor_copy(ident16[:], ident[:]).then_inc(pooled, 1)
                for n, (_, dst, g) in enumerate(units):
                    if g is None:
                        pool.wait_ge(split_hi, n + 1)
                        pool.tensor_tensor(dst[:, 1], stage[n], f(dst[:, 0]), ALU.subtract)\
                            .then_inc(split_lo[True], 1)

            @block.scalar
            def _(act):
                for n, (_, dst, _) in enumerate(units):
                    act.wait_ge(staged[n // 2], all_staged(n))
                    act.activation(dst[:, 0, :, 0:D], stage[n], ACT.Copy).then_inc(split_hi, 1)

            @block.vector
            def _(dve):
                step = 0

                def chain(ins):
                    nonlocal step
                    step += 1
                    ins.then_inc(made, 1)
                    dve.wait_ge(made, step)

                dve.wait_ge(adj_in, 32)
                dve.tensor_copy(adjt_f, adjt_i.bitcast(I32))
                chain(dve.tensor_copy(adj_f, adj_i.bitcast(I32)))
                dve.tensor_reduce(out=deg[:], in_=adj_f, axis=AX.X, op=ALU.add)
                dve.tensor_scalar(maskp[:], adj_f, 0.0, BIG, ALU.is_equal, ALU.mult)
                dve.tensor_scalar(mask3p[:], adj_f, 0.0, BIG, ALU.is_le, ALU.mult)
                dve.tensor_copy(at[:, 0], adjt_f)
                chain(dve.tensor_scalar(linked, adj_f, 0.0, None, ALU.not_equal))
                dve.tensor_tensor(at[:, 1], adjt_f, f(at[:, 0]), ALU.subtract)
                chain(dve.tensor_reduce(out=has[:], in_=linked, axis=AX.X, op=ALU.max))
                chain(dve.reciprocal(zz[0][:], has[:]))
                chain(dve.tensor_tensor(zz[0][:], zz[0][:], has[:], ALU.mult))
                dve.sem_inc(adjacency_made, 1)
                dve.wait_ge(vectors_in, 16 * (2 * len(avecs) + 2))
                for c in reversed(range(C)):
                    dve.tensor_scalar(degb[:, c, :], degb[:, 0, :], deg[:, c:c + 1], None, ALU.mult)
                    chain(dve.tensor_scalar(bo_nan[:, c, :], bo_nan[:, 0, :], zz[0][:, c:c + 1], None, ALU.mult))
                for n, (_, dst, g) in enumerate(units):
                    if g is None:
                        continue
                    dve.wait_ge(staged[n // 2], all_staged(n))
                    for c in range(C):
                        for k in range(2):
                            last = dve.tensor_tensor_reduce(
                                out=products[:, k, c, :], in0=stage[n][:, c, :], in1=avec[g][:, k, :],
                                scale=1.0 - 2.0 * k, scalar=0.0, op0=ALU.mult, op1=ALU.add,
                                accum_out=wcol[:, n, c, k:k + 1])
                    chain(last)
                    dve.wait_ge(split_hi, n + 1)
                    dve.tensor_tensor(dst[:, 1, :, 0:D], stage[n], f(dst[:, 0, :, 0:D]), ALU.subtract)\
                        .then_inc(split_lo[False], 1)
                    chain(dve.tensor_copy(dst[:, 0, :, D:WC], wcol[:, n, :, :]))
                    chain(dve.tensor_tensor(dst[:, 1, :, D:WC], wcol[:, n, :, :], f(dst[:, 0, :, D:WC]),
                                            ALU.subtract))

        TE, SC, VE, PO = range(4)
        HOP = ((0.0, 0.2, 0.2, 0.2), (0.22, 0.15, 0.15, 0.17), (0.25, 0.13, 0.13, 0.16), (0.16, 0.07, 0.06, 0.1))

        def product(a, name, k, cost, early, late):
            a(name + "_hi_part", k, TE, cost * 2 / 3, *early)
            a(name, k, TE, cost / 3, (name + "_hi_part", k), late)

        def norm_chain(a, n, t, src):
            a("stats", n, VE, 0.66, src)
            a("aggr", n, VE, 0.17, ("stats", n))
            a("var", n, VE, 0.08, ("aggr", n))
            a("inv_std", n, PO, 0.63, ("var", n))
            a("rows", n, VE, 0.47, ("inv_std", n))
            transposed(a, t, ("rows", n))

        def transposed(a, t, src):
            a("rows_T", t, TE, 0.43, src)
            a("rows_hi", t, SC, 0.48, ("rows_T", t))
            a("rows_lo", t, VE, 0.6, ("rows_hi", t))

        def graph_attention(a, g, src):
            if g == GOUT:
                a("cols", g, VE, 0.07, ("join", HG))
                a("spread", g, TE, 0.45, ("cols", g), ("tmin", g - 1))
            else:
                hi = ("rows_hi", src[1])
                product(a, "spread", g, 0.65, (hi, ("tmin", g - 1)), src)
                product(a, "wh", g, 1.3, (hi, ("wh_lo", g - 1)), src)
                a("cols", g, VE, 0.07, ("wh", g))
            a("wh_hi", g, SC, 0.48, ("cols", g), ("attend", g - HG))
            a("wh_lo", g, VE, 0.6, ("wh_hi", g))
            a("tmin", g, VE, 0.69, ("spread", g), *(("exps", 2 * g - 2 + c) for c in range(C)))
            a("top", g, VE, 0.08, ("tmin", g), ("cols", g))
            a("leaky_top", g, VE, 0.08, ("top", g))
            a("biases", g, VE, 0.16, ("leaky_top", g))
            for c in range(C):
                a("exps", C * g + c, SC, 0.8, ("biases", g), ("larger", C * g + c - C))
                a("larger", C * g + c, VE, 0.34, ("exps", C * g + c), ("probs_T", g - 1))
            a("inv_sum", g, VE, 0.08, *(("larger", C * g + c) for c in range(C)))
            if g:
                a("scale", g, *((PO, 1.1) if g < HG else (SC, 0.8)), ("inv_sum", g))
            a("probs_T", g, TE, 0.43, ("scale", g) if g else ("larger", C - 1), ("elu", g - 1))
            a("probs_hi", g, SC, 0.48, ("probs_T", g), ("attend", g - 1))
            a("probs_lo", g, VE, 0.6, ("probs_hi", g))
            if 1 <= g <= HG:
                a("attend", g, TE, 1.3, ("probs_lo", g), ("wh_lo", g))
            else:
                product(a, "attend", g, 1.3, (("probs_hi", g), ("wh_lo", g)), ("probs_lo", g))
            if g:
                a("elu_relu", g, SC, 0.48, ("attend", g), ("elu", g - 1))
                a("elu_exp", g, SC, 0.52, ("elu_relu", g))
                a("elu", g, VE, 0.6, ("elu_exp", g), ("hid_lo", g - 1))
            if 1 <= g <= HG:
                a("hid_hi", g, SC, 0.52, ("elu", g), ("join", g - 2))
                a("hid_lo", g, *((VE, 0.6) if g == HG else (PO, 1.23)), ("hid_hi", g))
                product(a, "join", g, 1.3, (("hid_hi", g), ("wh_lo", HG)), ("hid_lo", g))

        def front(a):
            a("x_deg", 0, PO, 1.23)
            norm_chain(a, 0, 0, None)
            product(a, "mj", 0, 1.3, (("rows_hi", 0),), ("rows_lo", 0))
            a("mi", 0, TE, 1.3, ("rows_lo", 0))
            a("mj_hi", 0, SC, 0.48, ("mj", 0))
            a("mj_lo", 0, VE, 0.6, ("mj_hi", 0))
            a("x_mi", 0, VE, 0.79, ("mi", 0), ("x_deg", 0))
            product(a, "amj", 0, 1.3, (("mj_hi", 0),), ("mj_lo", 0))
            a("x1", 0, VE, 0.6, ("amj", 0), ("x_mi", 0))
            norm_chain(a, 1, 1, ("x1", 0))
            graph_attention(a, 0, ("rows_lo", 1))
            a("x2", 0, VE, 0.79, ("attend", 0), ("inv_sum", 0))
            norm_chain(a, 2, 2, ("x2", 0))
            product(a, "q", 0, 1.3, (("rows_hi", 2),), ("rows_lo", 2))
            product(a, "k", 0, 1.3, (("q_hi_part", 0),), ("q", 0))
            a("v", 0, TE, 1.3, ("k", 0))
            a("q_full", 0, VE, 0.78, ("q", 0))
            a("q_hi", 0, SC, 0.52, ("q_full", 0))
            a("q_lo", 0, PO, 1.23, ("q_hi", 0))
            a("k_full", 0, SC, 0.72, ("k", 0))
            a("k_hi", 0, SC, 0.52, ("k_full", 0))
            a("k_lo", 0, VE, 0.6, ("k_hi", 0))
            a("v_full", 0, VE, 0.67, ("v", 0))
            a("v_a", 0, SC, 0.52, ("v_full", 0))
            a("v_r", 0, PO, 1.11, ("v_a", 0))
            a("v_b", 0, SC, 0.52, ("v_r", 0))
            a("v_c", 0, PO, 1.11, ("v_b", 0))
            for h in range(HQ):
                a("scores", h, TE, 0.66, ("q_lo", 0), ("k_lo", 0), ("smin", h - 2))
                a("smin", h, VE, 0.69, ("scores", h), ("s_exp", h - 2), ("v_r", 0) if h == 1 else None)
                a("s_exp", h, SC, 0.8, ("smin", h), ("p_lo", h - 2), ("v_c", 0) if h == 1 else None)
                a("p_hi", h, SC, 0.52, ("s_exp", h), ("p_T", h - 2))
                a("p_lo", h, PO, 1.11, ("p_hi", h))
                a("p_T_of_hi", h, TE, 0.22, ("p_hi", h), ("p_copy", h - 1) if h else ("v_full", 0))
                a("p_T", h, TE, 0.22, ("p_lo", h), ("p_T_of_hi", h))
                a("p_copy", h, VE, 0.6, ("p_T", h), ("values", h - 1))
                a("values", h, TE, 0.34, ("p_copy", h), ("v_c", 0), ("gather", h // 2 - 1) if h % 2 == 0 else ("values", h - 1))
                if h % 2:
                    a("gather", h // 2, VE, 0.53, ("values", h), ("normal", h // 2 - 1))
                    a("normal", h // 2, VE, 0.25, ("gather", h // 2))
            a("x_bo", 0, PO, 1.23, ("rows", 2), ("v_c", 0))
            transposed(a, TR_CTX, ("normal", HQ // 2 - 1))
            product(a, "wo", 0, 1.3, (("rows_hi", TR_CTX),), ("rows_lo", TR_CTX))
            a("x3", 0, VE, 0.6, ("wo", 0), ("x_bo", 0))

        def back(a):
            norm_chain(a, 3, 4, ("x3", 0))
            a("x_beta", 0, PO, 1.37, ("rows", 3))
            for g in range(1, HG + 1):
                graph_attention(a, g, ("rows_lo", 4))
            graph_attention(a, GOUT, ("rows_lo", 4))
            transposed(a, TR_OUT, ("elu", GOUT))
            a("out_b2", 0, PO, 1.37, ("rows_T", TR_OUT))
            product(a, "ffn1", 0, 1.3, (("rows_hi", TR_OUT),), ("rows_lo", TR_OUT))
            a("f1_full", 0, SC, 0.72, ("ffn1", 0))
            a("f1_hi", 0, SC, 0.52, ("f1_full", 0))
            a("f1_lo", 0, VE, 0.6, ("f1_hi", 0))
            product(a, "ffn2", 0, 1.3, (("f1_hi", 0),), ("f1_lo", 0))
            a("y", 0, VE, 0.6, ("ffn2", 0), ("out_b2", 0))
            a("stats", 4, VE, 0.66, ("y", 0))
            a("aggr", 4, VE, 0.17, ("stats", 4))
            a("var", 4, VE, 0.08, ("aggr", 4))
            a("inv_std", 4, PO, 0.63, ("var", 4))
            a("y_gamma", 0, VE, 0.79, ("aggr", 4))
            a("final", 0, VE, 0.79, ("y_gamma", 0), ("inv_std", 4), ("x_beta", 0))

        def arrange(chains):
            def hop(p, st):
                return 0.0 if p["step"][0] == st["step"][0] else HOP[p["engine"]][st["engine"]]

            todo = []
            for s, halves_of in chains:
                known, before = {}, None
                for n, half in enumerate(halves_of):
                    names, u = {}, n // 2

                    def a(name, k, engine, cost, *after):
                        todo.append(dict(step=(name, s, k, u), engine=engine, cost=cost, rest=0.0, at=None,
                                         after=after + ((name, k - 1),), before=before if len(names) < 2 else None))
                        names[(name, k)] = todo[-1]

                    half(a)
                    known.update(names)
                    for st in names.values():
                        st["after"] = [known[p] for p in st["after"] if p in known] \
                            + ([st["before"]] if st["before"] else [])
                    if half is back:
                        known, before = {}, names[("final", 0)]
            for st in reversed(todo):
                st["rest"] += st["cost"]
                for p in st["after"]:
                    p["rest"] = max(p["rest"], st["rest"] + hop(p, st))
            free, order = [0.0] * 4, []
            while todo:
                best = None
                for st in todo:
                    if all(p["at"] is not None for p in st["after"]):
                        start = max([free[st["engine"]]] + [p["at"] + p["cost"] + hop(p, st) for p in st["after"]])
                        key = (round(start / GRAIN), -st["rest"])
                        if best is None or key < best[0]:
                            best = (key, start, st)
                _, start, st = best
                st["at"] = start
                free[st["engine"]] = start + st["cost"]
                order.append(st["step"])
                todo.remove(st)
            return order

        GRAIN = 0.4
        def of(u, k, n):
            return u * n + k + 1

        def nth(s, k, front_n, n, u):
            return of(u, k if s == 0 else (k - front_n) % n, n)

        TR_CTX, TR_OUT = 3, 5
        def rows_bank(t):
            return BD if t in (1, 4, TR_OUT) else BC

        LN_TR = (0, 1, 2, 4)

        def row(s, t, u):
            return nth(s, t, 4, 6, u)

        def norm(s, n, u):
            return nth(s, n, 3, 5, u)

        def gat(s, g, u):
            return nth(s, g, 1, HG + 2, u)

        def gat_chunk(s, g, c, u):
            return C * (gat(s, g, u) - 1) + c + 1

        rows_ready, rows_T, rows_hi, rows_lo = (sem2(n) for n in ("rows_ready", "rows_T", "rows_hi", "rows_lo"))
        var_ready, rstd_ready = sem2("var_ready"), sem2("rstd_ready")
        deg_ready, bo_ready, beta_ready = sem2("deg_ready"), sem2("bo_ready"), sem2("beta_ready")
        mj_done, mi_done, mj_hi, mj_lo, amj_done = (sem2(n) for n in ("mj_done", "mi_done", "mj_hi", "mj_lo", "amj_done"))
        wh_done, cols_read, wh_hi, wh_lo = (sem2(n) for n in ("wh_done", "cols_read", "wh_hi", "wh_lo"))
        dbc_done, tmin_done, bias_ready, exp_done = sem2("dbc_done"), sem2("tmin_done"), sem2("bias_ready"), sem2("exp_done")
        larger_done, sum_ready, prob_ready = sem2("larger_done"), sem2("sum_ready"), sem2("prob_ready")
        joined = sem2("joined")
        pT_done, pT_hi, pT_lo, pv_done = sem2("pT_done"), sem2("pT_hi"), sem2("pT_lo"), sem2("pv_done")
        elu_relu, elu_exp, elu_done, hid_hi, hid_lo = (sem2(n) for n in ("elu_relu", "elu_exp", "elu_done", "hid_hi", "hid_lo"))
        qkv_done = sem2("qkv_done")
        q_full, q_hi, q_lo = sem2("q_full"), sem2("q_hi"), sem2("q_lo")
        k_full, k_hi, k_lo = sem2("k_full"), sem2("k_hi"), sem2("k_lo")
        v_full, v_a, v_r = sem2("v_full"), sem2("v_a"), sem2("v_r")
        v_b, v_c = sem2("v_b"), sem2("v_c")
        s_done, min_ready, p_done, p_hi, p_lo = (sem2(n) for n in ("s_done", "min_ready", "p_done", "p_hi", "p_lo"))
        p16_done, pT16_ready, o_done, o_used = (sem2(n) for n in ("p16_done", "pT16_ready", "o_done", "o_used"))
        wo_done = sem2("wo_done")
        f1_done, f1_full, f1_hi, f1_lo, f2_done = (sem2(n) for n in ("f1_done", "f1_full", "f1_hi", "f1_lo", "f2_done"))
        ob_ready, x_final = sem2("ob_ready"), sem2("x_final")
        loaded = sem2("loaded")
        vstep = sem("vstep")
        sems.append(vstep)
        nums = sorted(q.num for q in sems)
        assert nums == list(range(nums[0], nums[-1] + 1))

        def out_rows(b):
            return out[b].rearrange("(c p) d -> p c d", p=P)

        def run_steps(block, order, i):

            @block.sync
            def _(sp):
                if i is None:
                    sp.wait_ge(x_final[1], 1)
                    sp.dma_start(out_rows(B - 1), xs[1][:]).then_inc(stored[1], 16)
                    return
                for u in range(ROUNDS):
                    first = sp.snap((i * ROUNDS + u) * 2)
                    for s in S2:
                        nxt = sp.snap(((i * ROUNDS + u) * 2 + 2 + s) % B)
                        sp.wait_ge(rows_ready[s], row(s, 0, u))
                        sp.wait_ge(deg_ready[s], u + 1)
                        sp.dma_start(xin[s][:], x[nxt].rearrange("(c p) d -> p c d", p=P)).then_inc(loaded[s], 16)
                        o = 1 - s
                        sp.wait_ge(x_final[o], u + 1)
                        if o == 0:
                            sp.dma_start(out_rows(first), xs[0][:]).then_inc(stored[0], 16)
                        else:
                            before = sp.snap(((i * ROUNDS + u) * 2 + B - 1) % B)
                            sp.dma_start(out_rows(before), xs[1][:]).then_inc(stored[1], 16)
                for s in S2:
                    sp.wait_ge(loaded[s], 16 * ROUNDS)

            @block.gpsimd
            def _(pool):
                def inverse_std(s, n, u):
                    pool.wait_ge(var_ready[s], norm(s, n, u))
                    pool.tensor_tensor(rstd[s][:], ve[s][:], pow_half[:], ALU.pow).then_inc(rstd_ready[s], 1)

                def x_deg(s, _, u):
                    if s == 1 or u:
                        pool.wait_ge(x_final[s], u + s)
                    if u:
                        pool.wait_ge(loaded[s], 16 * u)
                    pool.tensor_tensor(e2[s][:], xin[s][:], degb[:], ALU.add).then_inc(deg_ready[s], 1)

                def scale(s, g, u):
                    if g >= HG:
                        return
                    pool.wait_ge(sum_ready[s], nth(s, g - 1, 0, HG + 1, u))
                    for c in range(C):
                        last = pool.tensor_scalar(pr[s][:, c, :], pr[s][:, c, :], rs[g % 2][s][:, c:c + 1], 1.0,
                                                  ALU.mult, ALU.mult)
                    last.then_inc(prob_ready[s], 1)

                def low_of_q(s, _, u):
                    pool.wait_ge(q_hi[s], u + 1)
                    pool.tensor_tensor(hid[s][:, 1, 0:C, :], fu[s][:], f(hid[s][:, 0, 0:C, :]), ALU.subtract)\
                        .then_inc(q_lo[s], 1)

                def value_rest(s, _, u):
                    pool.wait_ge(v_a[s], u + 1)
                    pool.tensor_tensor(e2[s][:], e1[s][:], v_part(s, 0), ALU.subtract).then_inc(v_r[s], 1)

                def value_third(s, _, u):
                    pool.wait_ge(v_b[s], u + 1)
                    pool.tensor_tensor(v_part(s, 2), as_heads(e2[s]), v_part(s, 1), ALU.subtract)\
                        .then_inc(v_c[s], 1)

                def x_bo(s, _, u):
                    pool.wait_ge(rows_ready[s], row(s, 2, u))
                    pool.tensor_tensor(xs[s][:], xs[s][:], bo_nan[:], ALU.add).then_inc(bo_ready[s], 1)

                def low_of_probs(s, h, u):
                    pool.wait_ge(p_hi[s], of(u, h, HQ))
                    pool.tensor_tensor(p16[s][h % 2][:, 1], l2_probs(s, h)[:], p16[s][h % 2][:, 0],
                                       ALU.subtract).then_inc(p_lo[s], 1)

                def x_beta(s, _, u):
                    pool.wait_ge(rows_ready[s], row(s, 4, u))
                    for c in range(C):
                        last = pool.tensor_tensor(xs[s][:, c, :], xs[s][:, c, :], beta_b[:], ALU.add)
                    last.then_inc(beta_ready[s], 1)

                def low_of_hidden(s, g, u):
                    if g == HG:
                        return
                    pool.wait_ge(hid_hi[s], of(u, g - 1, HG))
                    pool.tensor_tensor(hid_part(s, 1, g), fu[s][:], f(hid_part(s, 0, g)),
                                       ALU.subtract).then_inc(hid_lo[s], 1)

                def out_b2(s, _, u):
                    pool.wait_ge(rows_T[s], row(s, TR_OUT, u))
                    for c in range(C):
                        last = pool.tensor_tensor(fu[s][:, c, :], fu[s][:, c, :], b2_b[:], ALU.add)
                    last.then_inc(ob_ready[s], 1)

                program = dict(inv_std=inverse_std, x_deg=x_deg, scale=scale, q_lo=low_of_q, v_r=value_rest, v_c=value_third, x_bo=x_bo, p_lo=low_of_probs, x_beta=x_beta, hid_lo=low_of_hidden, out_b2=out_b2)
                for name, s, k, u in order:
                    if name in program:
                        program[name](s, k, u)

            @block.scalar
            def _(act):
                def high_of_rows(s, t, u):
                    act.wait_ge(rows_T[s], row(s, t, u))
                    act.activation(hT[s][:, 0], bank(s, rows_bank(t)),
                                   ACT.Relu if t in LN_TR else ACT.Copy).then_inc(rows_hi[s], 1)

                def high_of_mj(s, _, u):
                    act.wait_ge(mj_done[s], u + 1)
                    act.activation(whs[s][1][:, 0], bank(s, BA), ACT.Copy).then_inc(mj_hi[s], 1)

                def high_of_weights(s, g, u):
                    act.wait_ge(cols_read[s], gat(s, g, u))
                    act.activation(wh_parts(s, g)[:, 0], wh_banks(s)[:, :, 0:D], ACT.Copy).then_inc(wh_hi[s], 1)

                def exps(s, k, u):
                    g, c = k // C, k % C
                    act.wait_ge(bias_ready[s], gat(s, g, u))
                    if g >= 2:
                        act.wait_ge(larger_done[s], gat_chunk(s, g - 1, c, u))
                    act.activation(e1[s][:, c, :], tb[s][:, c, :], ACT.Exp,
                                   bias=bias1[g % 2][s][:, c:c + 1], scale=-1.0)
                    act.activation(e2[s][:, c, :], tb[s][:, c, :], ACT.Exp,
                                   bias=bias2[g % 2][s][:, c:c + 1], scale=-SLOPE[g]).then_inc(exp_done[s], 1)

                def scale_last(s, g, u):
                    if g < HG:
                        return
                    act.wait_ge(sum_ready[s], nth(s, g - 1, 0, HG + 1, u))
                    for c in range(C):
                        last = act.activation(pr[s][:, c, :], pr[s][:, c, :], ACT.Copy,
                                              scale=rs[g % 2][s][:, c:c + 1])
                    last.then_inc(prob_ready[s], 1)

                def high_of_attention(s, g, u):
                    act.wait_ge(pT_done[s], gat(s, g, u))
                    if g >= 2:
                        act.wait_ge(pv_done[s], gat(s, g - 1, u))
                    act.activation(pT[s][:, 0], bank(s, BD), ACT.Copy).then_inc(pT_hi[s], 1)

                def relu_of_negated(s, g, u):
                    act.wait_ge(pv_done[s], gat(s, g, u))
                    if g >= 2:
                        act.wait_ge(elu_done[s], of(u, g - 2, HG))
                    act.activation(rb[s][:], bank(s, BD if g < GOUT else BC), ACT.Relu, scale=-1.0)\
                        .then_inc(elu_relu[s], 1)

                def elu_exponential(s, g, u):
                    act.wait_ge(elu_relu[s], of(u, g - 1, GOUT))
                    act.activation(rb[s][:], rb[s][:], ACT.Exp, scale=-1.0).then_inc(elu_exp[s], 1)

                def high_of_q(s, _, u):
                    act.wait_ge(q_full[s], u + 1)
                    act.activation(hid[s][:, 0, 0:C, :], fu[s][:], ACT.Copy).then_inc(q_hi[s], 1)

                def whole_k(s, _, u):
                    act.wait_ge(qkv_done[s], of(u, 1, 3))
                    for c in range(C):
                        act.activation(rb[s][:, c, :], bank(s, BB)[:, c, :], ACT.Identity,
                                       bias=bk_c[:, c:c + 1]).then_inc(k_full[s], 1)

                def high_of_k(s, _, u):
                    act.wait_ge(k_full[s], C * (u + 1))
                    act.activation(hid[s][:, 0, C:2 * C, :], rb[s][:], ACT.Copy).then_inc(k_hi[s], 1)

                def value_first(s, _, u):
                    act.wait_ge(v_full[s], u + 1)
                    act.activation(v_part(s, 0), as_heads(e1[s]), ACT.Copy).then_inc(v_a[s], 1)

                def value_second(s, _, u):
                    act.wait_ge(v_r[s], u + 1)
                    act.activation(v_part(s, 1), as_heads(e2[s]), ACT.Copy).then_inc(v_b[s], 1)

                def softmax_exp(s, h, u):
                    act.wait_ge(min_ready[s], of(u, h, HQ))
                    if h == 1:
                        act.wait_ge(v_c[s], u + 1)
                    if h >= 2:
                        act.wait_ge(p_lo[s], of(u, h - 2, HQ))
                    for c in range(C):
                        last = act.activation(l2_probs(s, h)[:, c, :], l2_logits(s, h)[:, c, :], ACT.Exp,
                                              bias=hmin[s][h % 2][:, c:c + 1], scale=-1.0)
                    last.then_inc(p_done[s], 1)

                def high_of_probs(s, h, u):
                    act.wait_ge(p_done[s], of(u, h, HQ))
                    if h >= 2:
                        act.wait_ge(p16_done[s], of(u, h - 2, HQ))
                    act.activation(p16[s][h % 2][:, 0], l2_probs(s, h)[:], ACT.Copy).then_inc(p_hi[s], 1)

                def high_of_hidden(s, g, u):
                    act.wait_ge(elu_done[s], of(u, g - 1, HG))
                    if g > 2:
                        act.wait_ge(joined[s], of(u, g - 3, HG))
                    act.activation(hid_part(s, 0, g), fu[s][:], ACT.Copy).then_inc(hid_hi[s], 1)

                def whole_ffn(s, _, u):
                    act.wait_ge(f1_done[s], u + 1)
                    for c in range(C):
                        act.activation(rb[s][:, c, :], bank(s, BA)[:, c, :], ACT.Relu,
                                       bias=b1_c[:, c:c + 1]).then_inc(f1_full[s], 1)

                def high_of_ffn(s, _, u):
                    act.wait_ge(f1_full[s], C * (u + 1))
                    act.activation(hid[s][:, 0, 0:C, :], rb[s][:], ACT.Copy).then_inc(f1_hi[s], 1)

                program = dict(rows_hi=high_of_rows, mj_hi=high_of_mj, wh_hi=high_of_weights, exps=exps, scale=scale_last,
                               probs_hi=high_of_attention, elu_relu=relu_of_negated, elu_exp=elu_exponential,
                               q_hi=high_of_q, k_full=whole_k, k_hi=high_of_k, v_a=value_first,
                               v_b=value_second, s_exp=softmax_exp, p_hi=high_of_probs, hid_hi=high_of_hidden,
                               f1_full=whole_ffn, f1_hi=high_of_ffn)
                for name, s, k, u in order:
                    if name in program:
                        program[name](s, k, u)

            @block.tensor
            def _(pe):
                LEFT_FRESH = {False: ((0, 0), (0, 1)), True: ((1, 0),), None: PARTS}
                RIGHT_FRESH = {False: ((0, 0), (1, 0)), True: ((0, 1),), None: PARTS}

                def product(dst, lhs, rhs, terms, passes, low, opens=True, closes=True):
                    n = 0
                    for t in range(terms):
                        for a, b in passes[low]:
                            n += 1
                            last = pe.matmul(dst, lhs(a, t), rhs(b, t), start=(not low and opens and n == 1),
                                             stop=(low is not False and closes
                                                   and n == terms * len(passes[low])))
                    return last

                def blk(k):
                    return slice(k * P, (k + 1) * P)

                def one_bank(c, low):
                    return (low is None or c == 0), (low is None or c == C - 1)

                def rows_from(s, k, w, low):
                    for c in range(C):
                        last = product(bank(s, k)[:, c, :], lambda a, t: hT[s][:, a, t, blk(c)],
                                       lambda b, t: w[:, b, t, :], C, LEFT_FRESH, low,
                                       *one_bank(c, low))
                    return last

                def columns_from(s, k, w, low):
                    for c in range(C):
                        last = product(bank(s, k)[:, c, :], lambda a, t: w[:, a, t, blk(c)],
                                       lambda b, t: hT[s][:, b, t, :], C, RIGHT_FRESH, low,
                                       *one_bank(c, low))
                    return last

                def transpose_rows(s, t, u):
                    k = rows_bank(t)
                    src = pr if t in LN_TR else fu
                    pe.wait_ge(rows_ready[s], row(s, t, u))
                    for kc in range(C):
                        for c in range(C):
                            last = pe.transpose(bank(s, k)[:, kc, blk(c)], src[s][:, c, blk(kc)], ident[:])
                    last.then_inc(rows_T[s], 1)

                def layer0_neighbours(s, _, u, low):
                    if not low:
                        pe.wait_ge(rows_hi[s], row(s, 0, u))
                        rows_from(s, BA, w0[:, :, C:2 * C, :], low)
                    else:
                        pe.wait_ge(rows_lo[s], row(s, 0, u))
                        rows_from(s, BA, w0[:, :, C:2 * C, :], low).then_inc(mj_done[s], 1)

                def layer0_own(s, _, u):
                    pe.wait_ge(rows_lo[s], row(s, 0, u))
                    rows_from(s, BB, w0[:, :, 0:C, :], None).then_inc(mi_done[s], 1)

                def layer0_sum(s, _, u, low):
                    if not low:
                        pe.wait_ge(mj_hi[s], u + 1)
                    else:
                        pe.wait_ge(mj_lo[s], u + 1)
                    for c in range(C):
                        last = product(bank(s, BD)[:, c, :], lambda a, t: at[:, a, t, blk(c)],
                                       lambda b, t: whs[s][1][:, b, t, :], C, RIGHT_FRESH, low,
                                       *one_bank(c, low))
                    if low:
                        last.then_inc(amj_done[s], 1)

                def attention_weights(s, g, u, low):
                    if not low:
                        pe.wait_ge(rows_hi[s], row(s, 4 if g else 1, u))
                        if g >= 2:
                            pe.wait_ge(wh_lo[s], gat(s, g - 1, u))
                    else:
                        pe.wait_ge(rows_lo[s], row(s, 4 if g else 1, u))
                    w = layer1_or_head(g)
                    for c in range(C):
                        last = product(wh_banks(s)[:, c, 0:WC], lambda a, t: hT[s][:, a, t, blk(c)],
                                       lambda b, t: w[:, b, t, :], C, LEFT_FRESH, low)
                    if low:
                        last.then_inc(wh_done[s], 1)

                def join_head(s, g, u, low):
                    if not low:
                        pe.wait_ge(hid_hi[s], of(u, g - 1, HG))
                        if g == 1:
                            pe.wait_ge(wh_lo[s], gat(s, HG, u))
                    else:
                        pe.wait_ge(hid_lo[s], of(u, g - 1, HG))
                    for c in range(C):
                        n = 0
                        for t in range(C):
                            for a, b in LEFT_FRESH[low]:
                                n += 1
                                last = pe.matmul(wh_banks(s)[:, c, 0:WC], hid_part(s, a, g)[:, t, blk(c)],
                                                 wout[:, b, C * (g - 1) + t, :],
                                                 start=(g == 1 and not low and n == 1),
                                                 stop=(g == HG and low and n == C))
                    if low:
                        last.then_inc(joined[s], 1)

                def spread_targets(s, g, u, low):
                    if g >= 2 and not low:
                        pe.wait_ge(tmin_done[s], gat(s, g - 1, u))
                    if not low:
                        pe.wait_ge(rows_hi[s], row(s, 4 if g else 1, u))
                    else:
                        pe.wait_ge(rows_lo[s], row(s, 4 if g else 1, u))
                    w = layer1_or_head(g)
                    last = product(bank(s, BC)[:, 0, :], lambda a, t: w[:, a, t, D + 1:WC].broadcast_to([P, P]),
                                   lambda b, t: hT[s][:, b, t, :], C, RIGHT_FRESH, low)
                    if low:
                        last.then_inc(dbc_done[s], 1)

                def spread_output_targets(s, g, u):
                    pe.wait_ge(tmin_done[s], gat(s, g - 1, u))
                    pe.wait_ge(cols_read[s], gat(s, g, u))
                    for c in range(C):
                        last = pe.matmul(bank(s, BC)[:, 0, blk(c)], cols[g][s][:, c, 1:2].broadcast_to([P, P]),
                                         ident[:], start=True, stop=True)
                    last.then_inc(dbc_done[s], 1)

                def transpose_attention(s, g, u):
                    if g:
                        pe.wait_ge(prob_ready[s], nth(s, g - 1, 0, HG + 1, u))
                    else:
                        pe.wait_ge(larger_done[s], gat_chunk(s, 0, C - 1, u))
                    if g >= 2:
                        pe.wait_ge(elu_done[s], of(u, g - 2, HG))
                    for jc in range(C):
                        for c in range(C):
                            last = pe.transpose(bank(s, BD)[:, jc, blk(c)], pr[s][:, c, blk(jc)], ident[:])
                    last.then_inc(pT_done[s], 1)

                def attend_in_head(s, g, u):
                    pe.wait_ge(pT_lo[s], gat(s, g, u))
                    pe.wait_ge(wh_lo[s], gat(s, g, u))
                    w = wh_parts(s, g)
                    for c in range(C):
                        last = product(bank(s, BD)[:, c, :], lambda a, t: w[:, a, t, blk(c)],
                                       lambda b, t: pT[s][:, b, t, :], C, RIGHT_FRESH, None)
                    last.then_inc(pv_done[s], 1)

                def attend_in_rows(s, g, u, low):
                    if not low:
                        pe.wait_ge(pT_hi[s], gat(s, g, u))
                        pe.wait_ge(wh_lo[s], gat(s, g, u))
                    else:
                        pe.wait_ge(pT_lo[s], gat(s, g, u))
                    w = wh_parts(s, g)
                    for c in range(C):
                        last = product(bank(s, BC)[:, c, :], lambda a, t: pT[s][:, a, t, blk(c)],
                                       lambda b, t: w[:, b, t, :], C, LEFT_FRESH, low,
                                       *one_bank(c, low))
                    if low:
                        last.then_inc(pv_done[s], 1)

                def query(s, _, u, low):
                    if not low:
                        pe.wait_ge(rows_hi[s], row(s, 2, u))
                        columns_from(s, BA, wq, low)
                    else:
                        pe.wait_ge(rows_lo[s], row(s, 2, u))
                        columns_from(s, BA, wq, low).then_inc(qkv_done[s], 1)

                def key(s, _, u, low):
                    last = columns_from(s, BB, wk, low)
                    if low:
                        last.then_inc(qkv_done[s], 1)

                def value(s, _, u):
                    rows_from(s, BC, wv, None).then_inc(qkv_done[s], 1)

                def scores(s, h, u):
                    if h == 0:
                        pe.wait_ge(q_lo[s], u + 1)
                        pe.wait_ge(k_lo[s], u + 1)
                    if h >= 2:
                        pe.wait_ge(min_ready[s], of(u, h - 2, HQ))
                    r, oc = slice(DH * (h % 4), DH * (h % 4) + DH), h // 4
                    for c in range(C):
                        for n, (a, b) in enumerate(PARTS):
                            last = pe.matmul(bank(s, h % 2)[:, c, :], hid[s][r, a, oc, blk(c)],
                                             hid[s][r, b, C + oc, :], start=(n == 0), stop=(n == 2))
                    last.then_inc(s_done[s], 1)

                def transpose_part(s, h, part):
                    for kc in range(C):
                        for c in range(C):
                            last = pe.transpose(bank16(s, BC)[:, part, kc, blk(c)],
                                                p16[s][h % 2][:, part, c, blk(kc)], ident16[:])
                    return last

                def transpose_probs_hi(s, h, u):
                    pe.wait_ge(p_hi[s], of(u, h, HQ))
                    if h == 0:
                        pe.wait_ge(v_full[s], u + 1)
                    else:
                        pe.wait_ge(pT16_ready[s], of(u, h - 1, HQ))
                    transpose_part(s, h, 0)

                def transpose_probs_lo(s, h, u):
                    pe.wait_ge(p_lo[s], of(u, h, HQ))
                    transpose_part(s, h, 1).then_inc(p16_done[s], 1)

                def values(s, h, u):
                    pe.wait_ge(pT16_ready[s], of(u, h, HQ))
                    if h == 0:
                        pe.wait_ge(v_c[s], u + 1)
                    if h % 2 == 0 and h:
                        pe.wait_ge(o_used[s], of(u, h // 2 - 1, HQ // 2))
                    for c in range(C):
                        at0 = BD * BANK + ((h % 2) * C + c) * VC
                        for n, (part, kc) in enumerate(((0, 0), (0, 1), (1, 0), (1, 1))):
                            last = pe.matmul(ps[s][:, at0:at0 + VC], pT16[s][:, part, kc, blk(c)],
                                             v3[s][:, kc, h, :], start=(n == 0), stop=(n == 2 * C - 1))
                    last.then_inc(o_done[s], 1)

                def context_out(s, _, u, low):
                    if not low:
                        pe.wait_ge(rows_hi[s], row(s, TR_CTX, u))
                        rows_from(s, BA, wo, low)
                    else:
                        pe.wait_ge(rows_lo[s], row(s, TR_CTX, u))
                        rows_from(s, BA, wo, low).then_inc(wo_done[s], 1)

                def ffn_in(s, _, u, low):
                    if not low:
                        pe.wait_ge(rows_hi[s], row(s, TR_OUT, u))
                        columns_from(s, BA, wf1, low)
                    else:
                        pe.wait_ge(rows_lo[s], row(s, TR_OUT, u))
                        columns_from(s, BA, wf1, low).then_inc(f1_done[s], 1)

                def ffn_out(s, _, u, low):
                    if not low:
                        pe.wait_ge(f1_hi[s], u + 1)
                    else:
                        pe.wait_ge(f1_lo[s], u + 1)
                    for c in range(C):
                        last = product(bank(s, BB)[:, c, :], lambda a, t: hid[s][:, a, t, blk(c)],
                                       lambda b, t: wf2[:, b, t, :], C, LEFT_FRESH, low,
                                       *one_bank(c, low))
                    if low:
                        last.then_inc(f2_done[s], 1)

                program = dict(rows_T=transpose_rows, mi=layer0_own, probs_T=transpose_attention, v=value,
                               scores=scores, p_T_of_hi=transpose_probs_hi, p_T=transpose_probs_lo, values=values)
                of_some = {("spread", GOUT): spread_output_targets}
                of_some.update({("attend", g): attend_in_head for g in range(1, HG + 1)})
                in_two = dict(mj=layer0_neighbours, amj=layer0_sum, wh=attention_weights, join=join_head,
                              spread=spread_targets, attend=attend_in_rows, q=query, k=key, wo=context_out,
                              ffn1=ffn_in, ffn2=ffn_out)
                for name, s, k, u in order:
                    if name in program:
                        program[name](s, k, u)
                    elif (name, k) in of_some:
                        of_some[name, k](s, k, u)
                    elif name in in_two:
                        in_two[name](s, k, u, True)
                    elif name.removesuffix("_hi_part") in in_two:
                        in_two[name.removesuffix("_hi_part")](s, k, u, False)

            @block.vector
            def _(dve):
                marks = {}
                count = [0]

                def mark(ins, key):
                    count[0] += 1
                    ins.then_inc(vstep, 1)
                    marks[key] = count[0]

                def after(key):
                    if key in marks:
                        dve.wait_ge(vstep, marks[key])

                def norm_src(s, n):
                    return xin[s] if n == 0 else e1[s] if n == 4 else xs[s]

                def stats_of(s, n, u):
                    if n == 0 and u:
                        dve.wait_ge(loaded[s], 16 * u)
                    after(("y" if n == 4 else "x", s))
                    for c in range(C):
                        last = dve.bn_stats(stats[s][:, c, :], norm_src(s, n)[:, c, :])
                    mark(last, ("stats", s))

                def aggregate(s, n, u):
                    after(("stats", s))
                    for c in range(C):
                        last = dve.bn_aggr(mv[s][:, c, :], stats[s][:, c, :])
                    mark(last, ("aggr", s))

                def variance(s, n, u):
                    after(("aggr", s))
                    dve.tensor_scalar(ve[s][:], mv[s][:, :, 1], EPS, None, ALU.add).then_inc(var_ready[s], 1)

                def norm_rows(s, n, u):
                    dve.wait_ge(rstd_ready[s], norm(s, n, u))
                    for c in range(C):
                        last = dve.tensor_scalar(pr[s][:, c, :], norm_src(s, n)[:, c, :], mv[s][:, c, 0:1],
                                                 rstd[s][:, c:c + 1], ALU.subtract, ALU.mult)
                    last.then_inc(rows_ready[s], 1)

                def low_of_rows(s, t, u):
                    dve.wait_ge(rows_hi[s], row(s, t, u))
                    src = bank(s, rows_bank(t))
                    dst, hi = hT[s][:, 1], f(hT[s][:, 0])
                    if t in LN_TR:
                        ins = dve.scalar_tensor_tensor(out=dst, in0=src, scalar=0.0, in1=hi,
                                                       op0=ALU.max, op1=ALU.subtract)
                    else:
                        ins = dve.tensor_tensor(dst, src, hi, ALU.subtract)
                    ins.then_inc(rows_lo[s], 1)

                def low_of_mj(s, _, u):
                    dve.wait_ge(mj_hi[s], u + 1)
                    dve.tensor_tensor(whs[s][1][:, 1], bank(s, BA), f(whs[s][1][:, 0]), ALU.subtract)\
                        .then_inc(mj_lo[s], 1)

                def x_plus_own(s, _, u):
                    dve.wait_ge(stored[s], dve.snap((i * ROUNDS + u) * 16 + 16))
                    dve.wait_ge(mi_done[s], u + 1)
                    dve.wait_ge(deg_ready[s], u + 1)
                    for c in range(C):
                        last = dve.scalar_tensor_tensor(out=xs[s][:, c, :], in0=bank(s, BB)[:, c, :],
                                                        scalar=deg[:, c:c + 1], in1=e2[s][:, c, :],
                                                        op0=ALU.mult, op1=ALU.add)
                    mark(last, ("x", s))

                def x_plus(done, k):
                    def add(s, _, u):
                        dve.wait_ge(done[s], u + 1)
                        if k == BA:
                            dve.wait_ge(bo_ready[s], u + 1)
                        after(("x", s))
                        mark(dve.tensor_tensor(xs[s][:], xs[s][:], bank(s, k), ALU.add), ("x", s))
                    return add

                def source_and_target_columns(s, g, u):
                    if g == GOUT:
                        dve.wait_ge(joined[s], of(u, HG - 1, HG))
                    else:
                        dve.wait_ge(wh_done[s], nth(s, g, 1, HG + 1, u))
                    dve.tensor_copy(cols[g][s][:], wh_banks(s)[:, :, D:WC]).then_inc(cols_read[s], 1)

                def low_of_weights(s, g, u):
                    dve.wait_ge(wh_hi[s], gat(s, g, u))
                    dve.tensor_tensor(wh_parts(s, g)[:, 1], wh_banks(s)[:, :, 0:D],
                                      f(wh_parts(s, g)[:, 0]), ALU.subtract).then_inc(wh_lo[s], 1)

                def masked_minimum(s, g, u):
                    m = maskp if g == 0 else mask3p
                    dve.wait_ge(dbc_done[s], gat(s, g, u))
                    if g >= 2:
                        dve.wait_ge(exp_done[s], gat_chunk(s, g - 1, C - 1, u))
                    for c in range(C):
                        last = dve.tensor_tensor_reduce(
                            out=tb[s][:, c, :], in0=bank(s, BC)[:, 0, :], in1=m[:, c, :], scale=1.0,
                            scalar=3.0e38, op0=ALU.add, op1=ALU.min, accum_out=dmin[s][:, c:c + 1])
                    last.then_inc(tmin_done[s], 1)

                def top_logit(s, g, u):
                    dve.wait_ge(tmin_done[s], gat(s, g, u))
                    dve.wait_ge(cols_read[s], gat(s, g, u))
                    mark(dve.tensor_tensor(zz[s][:], cols[g][s][:, :, 0], dmin[s][:], ALU.subtract), ("zz", s))

                def leaky_top(s, g, u):
                    after(("zz", s))
                    mark(dve.scalar_tensor_tensor(out=mm[s][:], in0=zz[s][:], scalar=SLOPE[g], in1=zz[s][:],
                                                  op0=ALU.mult, op1=ALU.max), ("mm", s))

                def exp_biases(s, g, u):
                    after(("mm", s))
                    src = cols[g][s][:, :, 0]
                    mark(dve.tensor_tensor(bias1[g % 2][s][:], src, mm[s][:], ALU.subtract), ("bias", s))
                    dve.scalar_tensor_tensor(out=bias2[g % 2][s][:], in0=src, scalar=SLOPE[g], in1=mm[s][:],
                                             op0=ALU.mult, op1=ALU.subtract).then_inc(bias_ready[s], 1)

                def larger_branch(s, k, u):
                    g, c = k // C, k % C
                    dve.wait_ge(exp_done[s], gat_chunk(s, g, c, u))
                    if g >= 2:
                        dve.wait_ge(pT_done[s], gat(s, g - 1, u))
                    dve.scalar_tensor_tensor(out=pr[s][:, c, :], in0=e1[s][:, c, :], scalar=1.0,
                                             in1=e2[s][:, c, :], op0=ALU.mult, op1=ALU.max,
                                             accum_out=psums[s][:, c:c + 1]).then_inc(larger_done[s], 1)

                def inverse_sums(s, g, u):
                    dve.wait_ge(larger_done[s], gat_chunk(s, g, C - 1, u))
                    if g:
                        dve.reciprocal(rs[g % 2][s][:], psums[s][:]).then_inc(sum_ready[s], 1)
                    else:
                        mark(dve.reciprocal(rs[0][s][:], psums[s][:]), ("rs", s))
                        after(("rs", s))
                        mark(dve.tensor_tensor(rs[0][s][:], rs[0][s][:], has[:], ALU.mult), ("rs", s))

                def x_plus_attention(s, _, u):
                    dve.wait_ge(pv_done[s], gat(s, 0, u))
                    after(("x", s))
                    after(("rs", s))
                    for c in range(C):
                        last = dve.scalar_tensor_tensor(out=xs[s][:, c, :], in0=bank(s, BC)[:, c, :],
                                                        scalar=rs[0][s][:, c:c + 1], in1=xs[s][:, c, :],
                                                        op0=ALU.mult, op1=ALU.add)
                    mark(last, ("x", s))

                def low_of_attention(s, g, u):
                    dve.wait_ge(pT_hi[s], gat(s, g, u))
                    dve.tensor_tensor(pT[s][:, 1], bank(s, BD), f(pT[s][:, 0]), ALU.subtract)\
                        .then_inc(pT_lo[s], 1)

                def elu(s, g, u):
                    dve.wait_ge(elu_exp[s], of(u, g - 1, GOUT))
                    if g >= 2:
                        dve.wait_ge(hid_lo[s], of(u, g - 2, HG))
                    dve.scalar_tensor_tensor(out=fu[s][:], in0=rb[s][:], scalar=-1.0,
                                             in1=bank(s, BD if g < GOUT else BC), op0=ALU.add, op1=ALU.max)\
                        .then_inc(elu_done[s] if g < GOUT else rows_ready[s], 1)

                def low_of_last_head(s, g, u):
                    if g < HG:
                        return
                    dve.wait_ge(hid_hi[s], of(u, g - 1, HG))
                    dve.tensor_tensor(hid_part(s, 1, g), fu[s][:], f(hid_part(s, 0, g)), ALU.subtract)\
                        .then_inc(hid_lo[s], 1)

                def low_of_k(s, _, u):
                    dve.wait_ge(k_hi[s], u + 1)
                    dve.tensor_tensor(hid[s][:, 1, C:2 * C, :], rb[s][:], f(hid[s][:, 0, C:2 * C, :]),
                                      ALU.subtract).then_inc(k_lo[s], 1)

                def whole_q(s, _, u):
                    dve.wait_ge(qkv_done[s], of(u, 0, 3))
                    for c in range(C):
                        last = dve.tensor_scalar(fu[s][:, c, :], bank(s, BA)[:, c, :], bq_c[:, c:c + 1], -SCALE,
                                                 ALU.add, ALU.mult)
                    last.then_inc(q_full[s], 1)

                def whole_v(s, _, u):
                    dve.wait_ge(qkv_done[s], of(u, 2, 3))
                    for c in range(C):
                        last = dve.tensor_tensor(e1[s][:, c, :], bank(s, BC)[:, c, :], bv_b[:], ALU.add)
                    last.then_inc(v_full[s], 1)

                def score_minimum(s, h, u):
                    dve.wait_ge(s_done[s], of(u, h, HQ))
                    if h == 1:
                        dve.wait_ge(v_r[s], u + 1)
                    if h >= 2:
                        dve.wait_ge(p_done[s], of(u, h - 2, HQ))
                    for c in range(C):
                        last = dve.tensor_tensor_reduce(
                            out=l2_logits(s, h)[:, c, :], in0=bank(s, h % 2)[:, c, :], in1=maskp[:, c, :],
                            scale=1.0, scalar=3.0e38, op0=ALU.add, op1=ALU.min,
                            accum_out=hmin[s][h % 2][:, c:c + 1])
                    last.then_inc(min_ready[s], 1)

                def copy_probs(s, h, u):
                    dve.wait_ge(p16_done[s], of(u, h, HQ))
                    if h:
                        dve.wait_ge(o_done[s], of(u, h - 1, HQ))
                    dve.tensor_copy(pT16[s][:], bank16(s, BC)).then_inc(pT16_ready[s], 1)

                def two_heads(s, p):
                    return fu[s][:, :, 2 * p * DH:(2 * p + 2) * DH].rearrange("p c (h d) -> p h c d", h=2)

                def gather_values(s, p, u):
                    dve.wait_ge(o_done[s], of(u, 2 * p + 1, HQ))
                    after(("ctx", s))
                    o = ps[s][:, BD * BANK:BD * BANK + 2 * C * VC].rearrange("p (g v) -> p g v", v=VC)
                    mark(dve.reciprocal(rden[s][:], o[:, :, 3 * DH]), ("rden", s))
                    for hh in range(2):
                        last = dve.tensor_reduce(
                            out=two_heads(s, p)[:, hh], axis=AX.X, op=ALU.add,
                            in_=o[:, hh * C:hh * C + C, 0:3 * DH].rearrange("p c (t d) -> p c d t", t=3))
                    last.then_inc(o_used[s], 1)

                def normalise(s, p, u):
                    dve.wait_ge(o_used[s], of(u, p, HQ // 2))
                    for hh in range(2):
                        r = rden[s][:, hh * C:hh * C + C].rearrange("p (c o) -> p c o", o=1)
                        last = dve.tensor_tensor(two_heads(s, p)[:, hh], two_heads(s, p)[:, hh],
                                                 r.broadcast_to([P, C, DH]), ALU.mult)
                    if p == HQ // 2 - 1:
                        last.then_inc(rows_ready[s], 1)
                    else:
                        mark(last, ("ctx", s))

                def low_of_ffn(s, _, u):
                    dve.wait_ge(f1_hi[s], u + 1)
                    dve.tensor_tensor(hid[s][:, 1, 0:C, :], rb[s][:], f(hid[s][:, 0, 0:C, :]), ALU.subtract)\
                        .then_inc(f1_lo[s], 1)

                def ffn_sum(s, _, u):
                    dve.wait_ge(f2_done[s], u + 1)
                    dve.wait_ge(ob_ready[s], u + 1)
                    mark(dve.tensor_tensor(e1[s][:], fu[s][:], bank(s, BB), ALU.add), ("y", s))

                def times_gamma(s, _, u):
                    after(("aggr", s))
                    for c in range(C):
                        last = dve.scalar_tensor_tensor(out=e2[s][:, c, :], in0=e1[s][:, c, :],
                                                        scalar=mv[s][:, c, 0:1], in1=gamma_b[:],
                                                        op0=ALU.subtract, op1=ALU.mult)
                    mark(last, ("yg", s))

                def result(s, _, u):
                    dve.wait_ge(rstd_ready[s], norm(s, 4, u))
                    after(("yg", s))
                    dve.wait_ge(beta_ready[s], u + 1)
                    for c in range(C):
                        last = dve.scalar_tensor_tensor(out=xs[s][:, c, :], in0=e2[s][:, c, :],
                                                        scalar=rstd[s][:, c:c + 1], in1=xs[s][:, c, :],
                                                        op0=ALU.mult, op1=ALU.add)
                    last.then_inc(x_final[s], 1)

                program = dict(stats=stats_of, aggr=aggregate, var=variance, rows=norm_rows, rows_lo=low_of_rows,
                               mj_lo=low_of_mj, x_mi=x_plus_own, x1=x_plus(amj_done, BD),
                               cols=source_and_target_columns, wh_lo=low_of_weights, tmin=masked_minimum, top=top_logit, leaky_top=leaky_top,
                               biases=exp_biases, larger=larger_branch, inv_sum=inverse_sums,
                               probs_lo=low_of_attention, elu=elu,
                               x2=x_plus_attention, hid_lo=low_of_last_head,
                               q_full=whole_q, k_lo=low_of_k, v_full=whole_v,
                               smin=score_minimum, p_copy=copy_probs, gather=gather_values, normal=normalise,
                               x3=x_plus(wo_done, BA), f1_lo=low_of_ffn, y=ffn_sum,
                               y_gamma=times_gamma, final=result)
                for name, s, k, u in order:
                    if name in program:
                        program[name](s, k, u)

        order = arrange(((0, (front, back) * ROUNDS), (1, (back, front) * ROUNDS)))
        with nc.Fori(0, LOOPS) as i:
            with nc.Block(no_gpsimd_drain=True) as block:
                run_steps(block, order, i)
            nc.all_engine_barrier(sems_to_clear=range(nums[0], nums[-1] + 1))

        with nc.Block() as block:
            run_steps(block, arrange(((1, (back,)),)), None)
        with nc.Block() as block:
            @block.sync
            def _(sp):
                sp.wait_ge(stored[0], 16 * (B // 2) + 16)
                sp.wait_ge(stored[1], 16 * (B // 2) + 16)


def kernel(**inputs):
    import numpy as np
    import concourse.bacc as bacc
    from concourse import mybir as _mybir
    from concourse.bass_utils import run_bass_kernel_spmd

    def t(a):
        return np.ascontiguousarray(np.asarray(a).T)

    g = {k: np.ascontiguousarray(np.asarray(v)) for k, v in inputs.items()}
    arrays = {
        "x_in": g["x"], "adj": g["adj"], "adj_t": t(g["adj"]),
        "L0_W_t": t(g["L0_gnn_W"]), "L0_b": g["L0_gnn_b"],
        "L1_W": g["L1_gnn_W"], "L1_a_src": g["L1_gnn_a_src"], "L1_a_dst": g["L1_gnn_a_dst"],
        "Wq_t": t(g["L2_gnn_Wq"]), "bq": g["L2_gnn_bq"], "Wk_t": t(g["L2_gnn_Wk"]), "bk": g["L2_gnn_bk"],
        "Wv_t": t(g["L2_gnn_Wv"]), "bv": g["L2_gnn_bv"], "Wo_t": t(g["L2_gnn_Wo"]), "bo": g["L2_gnn_bo"],
        "W_heads": g["L3_gnn_W_heads"], "a_heads": g["L3_gnn_a_heads"], "W_out": g["L3_gnn_W_out"],
        "a_out": g["L3_gnn_a_out"], "w1": g["L3_gnn_w1"], "b1": g["L3_gnn_b1"], "w2": g["L3_gnn_w2"],
        "b2": g["L3_gnn_b2"], "gamma": g["L3_gnn_ln_gamma"], "beta": g["L3_gnn_ln_beta"],
    }
    nc = bacc.Bacc("TRN2", target_bir_lowering=False, num_devices=1)
    args = [nc.dram_tensor(k, a.shape, _mybir.dt.from_np(a.dtype), kind="ExternalInput").ap()
            for k, a in arrays.items()]
    out = nc.dram_tensor("out", g["x"].shape, _mybir.dt.float32, kind="ExternalOutput").ap()
    adj_preln_kernel(nc, *args, out)
    r = run_bass_kernel_spmd(nc, [arrays], core_ids=[0])
    return r.results[0]["out"]
```
